# Optimizing a Trainium2 kernel written in Bass

```python
import numpy as np
import jax
import jax.numpy as jnp

def _softmax(x, axis=-1):
    return jax.nn.softmax(x, axis=axis)

def _gelu(x):
    return jax.nn.gelu(x, approximate=True)

def _silu(x):
    return jax.nn.silu(x)

def _sigmoid(x):
    return jax.nn.sigmoid(x)

def _layernorm(x, axis=-1, eps=1e-05):
    m = jnp.mean(x, axis=axis, keepdims=True)
    v = jnp.var(x, axis=axis, keepdims=True)
    return (x - m) / jnp.sqrt(v + eps)

def _scatter_add(tgt, idx, src, axis=0):
    return tgt.at[idx].add(src)

def _segment_sum(src, seg, n):
    return jax.ops.segment_sum(src, seg, n)
kernel_name = 'mk_seq_postln_d1_jaxref_r4_e7b352'

def setup_inputs(seed: int=0):
    np.random.seed(seed)
    _w = jnp.asarray

    def _L0_attn_setup():
        import jax, jax.numpy as jnp
        import numpy as np
        import math
        B, T, C = (64, 128, 256)
        LAYER_ID, N_LAYER = (6, 12)

        def _wkv(w, u, k, v):
            b, t, c = k.shape

            def step(carry, kv):
                aa, bb, pp = carry
                kt, vt = kv
                ww = u + kt
                q = jnp.maximum(pp, ww)
                e1 = jnp.exp(pp - q)
                e2 = jnp.exp(ww - q)
                y = (e1 * aa + e2 * vt) / (e1 * bb + e2)
                ww2 = pp + w
                q2 = jnp.maximum(ww2, kt)
                e1 = jnp.exp(ww2 - q2)
                e2 = jnp.exp(kt - q2)
                return ((e1 * aa + e2 * vt, e1 * bb + e2, q2), y)
            init = (jnp.zeros((b, c), k.dtype), jnp.zeros((b, c), k.dtype), jnp.full((b, c), -1e+38, k.dtype))
            _, ys = jax.lax.scan(step, init, (jnp.swapaxes(k, 0, 1), jnp.swapaxes(v, 0, 1)))
            return jnp.swapaxes(ys, 0, 1)
        key = jax.random.key(seed)
        k1, k2, k3, k4, k5 = jax.random.split(key, 5)
        r01 = LAYER_ID / N_LAYER
        r10 = 1.0 - r01
        i = jnp.arange(C, dtype=jnp.float32)
        ddd = i / C
        time_decay = -5.0 + 8.0 * (i / (C - 1)) ** (0.7 + 1.3 * r01)
        zigzag = ((jnp.arange(C) + 1) % 3 - 1).astype(jnp.float32) * 0.5
        time_first = jnp.full((C,), math.log(0.3), jnp.float32) + zigzag
        time_mix_k = (ddd ** r10).reshape(1, 1, C)
        time_mix_v = (ddd ** r10 + 0.3 * r01).reshape(1, 1, C)
        time_mix_r = (ddd ** (0.5 * r10)).reshape(1, 1, C)
        x = jax.random.normal(k1, (B, T, C), jnp.float32)
        Wk = jax.random.normal(k2, (C, C), jnp.float32) * 0.02
        Wv = jax.random.normal(k3, (C, C), jnp.float32) * 0.02
        Wr = jax.random.normal(k4, (C, C), jnp.float32) * 0.02
        Wo = jax.random.normal(k5, (C, C), jnp.float32) * 0.02
        return {'x': x, 'time_decay': time_decay, 'time_first': time_first, 'time_mix_k': time_mix_k, 'time_mix_v': time_mix_v, 'time_mix_r': time_mix_r, 'Wk': Wk, 'Wv': Wv, 'Wr': Wr, 'Wo': Wo}
    _L0_attn_in = _L0_attn_setup()

    def _L0_ffn_setup():
        import jax, jax.numpy as jnp
        import numpy as np
        DIM = 256
        HIDDEN = 768
        SCALE = 1.0 / 127.0

        def _dequant(w_int, dtype):
            return w_int.astype(dtype) * jnp.asarray(SCALE, dtype)
        key = jax.random.key(seed)
        k_x, k_g, k_u, k_d = jax.random.split(key, 4)
        x = jax.random.normal(k_x, (4, 512, DIM), dtype=jnp.float32)
        w_gate = jax.random.randint(k_g, (HIDDEN, DIM), -127, 128, dtype=jnp.int32)
        w_up = jax.random.randint(k_u, (HIDDEN, DIM), -127, 128, dtype=jnp.int32)
        w_down = jax.random.randint(k_d, (DIM, HIDDEN), -127, 128, dtype=jnp.int32)
        return {'x': x, 'w_gate': w_gate, 'w_up': w_up, 'w_down': w_down}
    _L0_ffn_in = _L0_ffn_setup()
    _d = {'L0_attn_x': _L0_attn_in['x'], 'L0_attn_time_decay': _L0_attn_in['time_decay'], 'L0_attn_time_first': _L0_attn_in['time_first'], 'L0_attn_time_mix_k': _L0_attn_in['time_mix_k'], 'L0_attn_time_mix_v': _L0_attn_in['time_mix_v'], 'L0_attn_time_mix_r': _L0_attn_in['time_mix_r'], 'L0_attn_Wk': _L0_attn_in['Wk'], 'L0_attn_Wv': _L0_attn_in['Wv'], 'L0_attn_Wr': _L0_attn_in['Wr'], 'L0_attn_Wo': _L0_attn_in['Wo'], 'L0_ffn_w_gate': _L0_ffn_in['w_gate'], 'L0_ffn_w_up': _L0_ffn_in['w_up'], 'L0_ffn_w_down': _L0_ffn_in['w_down']}
    _x0 = _d['L0_attn_x']
    _d['L0_attn_x'] = jax.random.normal(jax.random.fold_in(jax.random.key(seed), 1), (1, 4096, 256), dtype=_x0.dtype)
    del _x0
    return _d

def reference(L0_attn_x, L0_attn_time_decay, L0_attn_time_first, L0_attn_time_mix_k, L0_attn_time_mix_v, L0_attn_time_mix_r, L0_attn_Wk, L0_attn_Wv, L0_attn_Wr, L0_attn_Wo, L0_ffn_w_gate, L0_ffn_w_up, L0_ffn_w_down):

    def _L0_attn_ref(x, time_decay, time_first, time_mix_k, time_mix_v, time_mix_r, Wk, Wv, Wr, Wo):
        import jax, jax.numpy as jnp
        import numpy as np
        import math
        B, T, C = (64, 128, 256)
        LAYER_ID, N_LAYER = (6, 12)

        def _wkv(w, u, k, v):
            b, t, c = k.shape

            def step(carry, kv):
                aa, bb, pp = carry
                kt, vt = kv
                ww = u + kt
                q = jnp.maximum(pp, ww)
                e1 = jnp.exp(pp - q)
                e2 = jnp.exp(ww - q)
                y = (e1 * aa + e2 * vt) / (e1 * bb + e2)
                ww2 = pp + w
                q2 = jnp.maximum(ww2, kt)
                e1 = jnp.exp(ww2 - q2)
                e2 = jnp.exp(kt - q2)
                return ((e1 * aa + e2 * vt, e1 * bb + e2, q2), y)
            init = (jnp.zeros((b, c), k.dtype), jnp.zeros((b, c), k.dtype), jnp.full((b, c), -1e+38, k.dtype))
            _, ys = jax.lax.scan(step, init, (jnp.swapaxes(k, 0, 1), jnp.swapaxes(v, 0, 1)))
            return jnp.swapaxes(ys, 0, 1)
        xx = jnp.pad(x, ((0, 0), (1, 0), (0, 0)))[:, :-1]
        xk = x * time_mix_k + xx * (1.0 - time_mix_k)
        xv = x * time_mix_v + xx * (1.0 - time_mix_v)
        xr = x * time_mix_r + xx * (1.0 - time_mix_r)
        k = jnp.einsum('btc,dc->btd', xk, Wk)
        v = jnp.einsum('btc,dc->btd', xv, Wv)
        sr = jax.nn.sigmoid(jnp.einsum('btc,dc->btd', xr, Wr))
        w = -jnp.exp(time_decay)
        rwkv = sr * _wkv(w, time_first, k, v)
        return jnp.einsum('btc,dc->btd', rwkv, Wo)

    def _L0_ffn_ref(x, w_gate, w_up, w_down):
        import jax, jax.numpy as jnp
        import numpy as np
        DIM = 256
        HIDDEN = 768
        SCALE = 1.0 / 127.0

        def _dequant(w_int, dtype):
            return w_int.astype(dtype) * jnp.asarray(SCALE, dtype)
        wg = _dequant(w_gate, x.dtype)
        wu = _dequant(w_up, x.dtype)
        wd = _dequant(w_down, x.dtype)
        gate = jnp.einsum('bsd,hd->bsh', x, wg)
        up = jnp.einsum('bsd,hd->bsh', x, wu)
        h = jax.nn.silu(gate) * up
        return jnp.einsum('bsh,dh->bsd', h, wd)
    x = L0_attn_x
    x = _layernorm(x + _L0_attn_ref(x, L0_attn_time_decay, L0_attn_time_first, L0_attn_time_mix_k, L0_attn_time_mix_v, L0_attn_time_mix_r, L0_attn_Wk, L0_attn_Wv, L0_attn_Wr, L0_attn_Wo), axis=-1)
    x = _layernorm(x + _L0_ffn_ref(x, L0_ffn_w_gate, L0_ffn_w_up, L0_ffn_w_down), axis=-1)
    return x

_drawn_inputs = setup_inputs


def setup_inputs(seed=0):
    import zlib

    import numpy as np

    out = dict(_drawn_inputs(seed))
    spreads = {}
    factors = {'L0_attn_time_first': 8.0,
     'L0_attn_time_mix_k': 8.0,
     'L0_attn_time_mix_v': 5.546,
     'L0_attn_time_mix_r': 8.0,
     'L0_attn_Wk': 8.0,
     'L0_attn_Wr': 8.0}
    for name, (base, spread) in spreads.items():
        noise = np.random.default_rng([zlib.crc32(name.encode()), seed]).standard_normal(out[name].shape)
        drawn = base * np.exp(spread * noise) if base else spread * noise
        out[name] = jnp.asarray(drawn.astype(out[name].dtype))
    for name, factor in factors.items():
        out[name] = (out[name] * factor).astype(out[name].dtype)
    return out
```

```python
import concourse.bass as bass
from concourse import mybir
from contextlib import ExitStack


def rwkv_swiglu_kernel(nc: bass.Bass, xT: bass.AP, x: bass.AP, params: bass.AP, wk: bass.AP, wv: bass.AP,
                       wr: bass.AP, wo: bass.AP, wg: bass.AP, wu: bass.AP, wd: bass.AP, out: bass.AP):
    f32 = mybir.dt.float32
    f32r = mybir.dt.float32r
    i32 = mybir.dt.int32
    ALU = mybir.AluOpType
    ACT = mybir.ActivationFunctionType

    P = 128
    T, C = x.shape
    H = wd.shape[0]
    N = 512
    NC = T // N
    CH = C // P
    NT = N // P
    NM = H // P
    NH = 3
    SCALE = 1.0 / 127.0
    EPS = 1e-5
    START = -1e38
    DECAY, FIRST, MIX_K, MIX_R, MIX_V = range(5)
    MIX = [MIX_K, MIX_R, MIX_V]
    IN_NEW, IN_OLD, OUT_OLD, OUT_NEW = range(4)

    xT_v = xT.rearrange("(h p) t -> p h t", p=P)
    x_v = x.rearrange("(n p) c -> p n c", p=P)
    out_v = out.rearrange("(n p) c -> p n c", p=P)

    ctx = ExitStack()
    with ctx:
        def sb(name, shape, dt=f32):
            return ctx.enter_context(nc.sbuf_tensor(name, shape, dt))

        def ps(name, shape):
            return ctx.enter_context(nc.psum_tensor(name, shape, f32))

        def sem(name):
            return ctx.enter_context(nc.semaphore(name))

        xt = sb("xt", [P, CH, N + 1])
        xrow = sb("xrow", [P, NT, C])
        par = sb("par", [P, 5, CH])
        decay = sb("decay", [P, CH])
        neg_decay = sb("neg_decay", [P, CH])
        eps = sb("eps", [P, 1])
        wkT = sb("wkT", [P, CH, C])
        wrT = sb("wrT", [P, CH, C])
        wvT = sb("wvT", [P, CH, C])
        woT = sb("woT", [P, CH, C])
        wg_i = sb("wg_i", [P, CH, H], i32)
        wu_i = sb("wu_i", [P, CH, H], i32)
        wd_i = sb("wd_i", [P, NM, C], i32)
        wg_r = sb("wg_r", [P, CH, H], f32r)
        wu_r = sb("wu_r", [P, CH, H], f32r)
        wd_r = sb("wd_r", [P, NM, C], f32r)
        ident = sb("ident", [P, P])
        dx = sb("dx", [P, CH, N])
        mix = sb("mix", [P, 3, CH, N])
        pmax = sb("pmax", [P, CH, N + 1])
        state = sb("state", [P, 2, CH, N + 1])
        gap = sb("gap", [P, CH, N])
        wts = sb("wts", [P, 4, CH, N])
        kv = sb("kv", [P, CH, N])
        num = sb("num", [P, CH, N])
        num2 = sb("num2", [P, CH, N])
        den = sb("den", [P, CH, N])
        rec = sb("rec", [P, CH, N])
        recv = sb("recv", [P, CH, N])
        rwkv = sb("rwkv", [P, CH, N])
        res1 = sb("res1", [P, NT, C])
        stats1 = sb("stats1", [P, NT, 6])
        mv1 = sb("mv1", [P, NT, 2])
        lnv1 = sb("lnv1", [P, NT])
        rstd1 = sb("rstd1", [P, NT])
        x1 = sb("x1", [P, NT, C])
        x1hi = sb("x1hi", [P, CH, N], f32r)
        x1lo = sb("x1lo", [P, CH, N], f32r)
        act = sb("act", [P, 2, N])
        hid = sb("hid", [P, NH, N])
        hhi = sb("hhi", [P, NM, N], f32r)
        hlo = sb("hlo", [P, NM, N], f32r)
        res2 = sb("res2", [P, NT, C])
        stats2 = sb("stats2", [P, NT, 6])
        mv2 = sb("mv2", [P, NT, 2])
        lnv2 = sb("lnv2", [P, NT])
        rstd2 = sb("rstd2", [P, NT])
        shift2 = sb("shift2", [P, NT])
        y = sb("y", [P, NT, C])

        bank_a = ps("bank_a", [P, 2, N])
        bank_b = ps("bank_b", [P, 2, N])
        bank_c = ps("bank_c", [P, 2, N])
        bank_d = ps("bank_d", [P, 2, N])
        attn = bank_a[:, :, :].rearrange("p b (n c) -> p (b n) c", c=C)
        ffn = bank_c[:, :, :].rearrange("p b (n c) -> p (b n) c", c=C)

        par_in = sem("par_in")
        proj_in = sem("proj_in")
        wo_in = sem("wo_in")
        ffn_in = sem("ffn_in")
        xt_in = sem("xt_in")
        xrow_in = sem("xrow_in")
        stored = sem("stored")
        decay_exp = sem("decay_exp")
        decay_ready = sem("decay_ready")
        consts_ready = sem("consts_ready")
        ident_zero = sem("ident_zero")
        ident_ready = sem("ident_ready")
        state_zero = sem("state_zero")
        ffn_w_ready = sem("ffn_w_ready")
        dx_ready = sem("dx_ready")
        dx_scaled = sem("dx_scaled")
        mixed = sem("mixed")
        k_ready = sem("k_ready")
        r_ready = sem("r_ready")
        v_ready = sem("v_ready")
        pmax_carried = sem("pmax_carried")
        pmax_ready = sem("pmax_ready")
        gap_ready = sem("gap_ready")
        args_ready = sem("args_ready")
        wts_ready = sem("wts_ready")
        state_carried = sem("state_carried")
        bb_ready = sem("bb_ready")
        kv_ready = sem("kv_ready")
        aa_ready = sem("aa_ready")
        den_part = sem("den_part")
        den_ready = sem("den_ready")
        num_parts = sem("num_parts")
        num_ready = sem("num_ready")
        ln_ready = sem("ln_ready")
        rec_ready = sem("rec_ready")
        recv_ready = sem("recv_ready")
        gated = sem("gated")
        rwkv_ready = sem("rwkv_ready")
        attn_ready = sem("attn_ready")
        res1_ready = sem("res1_ready")
        stats1_ready = sem("stats1_ready")
        mv1_ready = sem("mv1_ready")
        lnv1_ready = sem("lnv1_ready")
        rstd1_ready = sem("rstd1_ready")
        x1_ready = sem("x1_ready")
        x1T_ready = sem("x1T_ready")
        x1hi_ready = sem("x1hi_ready")
        x1lo_ready = sem("x1lo_ready")
        gate_ready = sem("gate_ready")
        up_ready = sem("up_ready")
        act_ready = sem("act_ready")
        hid_ready = sem("hid_ready")
        hhi_ready = sem("hhi_ready")
        hlo_ready = sem("hlo_ready")
        ffn_ready = sem("ffn_ready")
        res2_ready = sem("res2_ready")
        stats2_ready = sem("stats2_ready")
        mv2_ready = sem("mv2_ready")
        lnv2_ready = sem("lnv2_ready")
        rstd2_ready = sem("rstd2_ready")
        shift2_ready = sem("shift2_ready")
        y_ready = sem("y_ready")

        block = ctx.enter_context(nc.Block())

        def first(c):
            return isinstance(c, int) and c == 0

        @block.sync
        def _(sp):
            def load_xt(c):
                if not first(c):
                    sp.wait_ge(mixed, c * (3 * CH))
                sp.dma_start(xt[:, :, :], xT_v[:, :, bass.ds(c * N, N + 1)]).then_inc(xt_in, 16)

            def load_xrow(c):
                if not first(c):
                    sp.wait_ge(res1_ready, c * 2)
                sp.dma_start(xrow[:, :, :], x_v[:, bass.ds(c * NT, NT), :]).then_inc(xrow_in, 16)

            def store(c):
                sp.wait_ge(y_ready, c * NT + NT)
                sp.dma_start(out_v[:, bass.ds(c * NT, NT), :], y[:, :, :]).then_inc(stored, 16)

            load_xt(0)
            sp.dma_start(wkT[:, :, :], wk.rearrange("(h p) d -> p h d", p=P)).then_inc(proj_in, 16)
            sp.dma_start(wrT[:, :, :], wr.rearrange("(h p) d -> p h d", p=P)).then_inc(proj_in, 16)
            sp.dma_start(wvT[:, :, :], wv.rearrange("(h p) d -> p h d", p=P)).then_inc(proj_in, 16)
            load_xrow(0)
            sp.dma_start(woT[:, :, :], wo.rearrange("(h p) d -> p h d", p=P)).then_inc(wo_in, 16)
            load_xt(1)
            load_xrow(1)
            with sp.Fori(2, NC) as c:
                load_xt(c)
                store(c - 2)
                load_xrow(c)
            store(NC - 2)
            store(NC - 1)
            sp.wait_ge(stored, 16 * NC)

        @block.gpsimd
        def _(pool):
            def diff(c, h):
                if h == 0:
                    pool.wait_ge(xt_in, c * 16 + 16)
                nc.gpsimd.tensor_tensor(dx[:, h, :], xt[:, h, 1:N + 1], xt[:, h, 0:N],
                                        ALU.subtract).then_inc(dx_ready, 1)

            def mixing(c, i, h):
                pool.wait_ge(dx_scaled, c * (3 * CH) + (i * CH + h + 1))
                nc.gpsimd.tensor_tensor(mix[:, i, h, :], mix[:, i, h, :], xt[:, h, 0:N],
                                        ALU.add).then_inc(mixed, 1)

            def numerator(c, h):
                pool.wait_ge(num_parts, c * CH + (h + 1))
                nc.gpsimd.tensor_tensor(num[:, h, :], num[:, h, :], num2[:, h, :],
                                        ALU.add).then_inc(num_ready, 1)

            def low_part(c, m):
                pool.wait_ge(hhi_ready, c * NM + (m + 1))
                if not first(c):
                    pool.wait_ge(ffn_ready, c * 2)
                nc.gpsimd.tensor_tensor(hlo[:, m, :], hid[:, m % NH, :], hhi[:, m, :].bitcast(f32),
                                        ALU.subtract).then_inc(hlo_ready, 1)

            def round_(j, ffn, nxt):
                if nxt:
                    diff(j + 1, 0)
                    diff(j + 1, 1)
                for m in range(NM):
                    if ffn:
                        low_part(j - 1, m)
                    if nxt and m in (1, 2):
                        mixing(j + 1, 0, m - 1)
                numerator(j, 0)
                numerator(j, 1)
                if nxt:
                    for i in range(1, 3):
                        mixing(j + 1, i, 0)
                        mixing(j + 1, i, 1)

            nc.gpsimd.dma_start(par[:, :, :], params).then_inc(par_in, 16)
            nc.gpsimd.dma_start(wg_i[:, :, :], wg.rearrange("(h p) n -> p h n", p=P)).then_inc(ffn_in, 16)
            nc.gpsimd.dma_start(wu_i[:, :, :], wu.rearrange("(h p) n -> p h n", p=P)).then_inc(ffn_in, 16)
            nc.gpsimd.dma_start(wd_i[:, :, :], wd.rearrange("(m p) c -> p m c", p=P)).then_inc(ffn_in, 16)
            diff(0, 0)
            diff(0, 1)
            for i in range(3):
                mixing(0, i, 0)
                mixing(0, i, 1)
            nc.gpsimd.memset(ident[:, :], 0.0).then_inc(ident_zero, 1)
            pool.wait_ge(ident_zero, 1)
            nc.gpsimd.affine_select(out=ident[:, :], in_=ident[:, :], compare_op=ALU.not_equal, fill=1.0, base=0,
                                    pattern=[[-1, P]], channel_multiplier=1).then_inc(ident_ready, 1)
            round_(0, False, True)
            round_(1, True, True)
            with pool.Fori(2, NC - 1) as j:
                round_(j, True, True)
            round_(NC - 1, True, False)
            for m in range(NM):
                low_part(NC - 1, m)

        @block.scalar
        def _(sc):
            def weight(c, i, h):
                sc.wait_ge(args_ready, c * (4 * CH) + (h * 4 + i + 1))
                old = i in (IN_OLD, OUT_OLD)
                nc.scalar.activation(wts[:, i, h, :], wts[:, i, h, :], ACT.Exp,
                                     scale=-1.0 if old else 1.0).then_inc(wts_ready, 1)

            def scale_dx(c, i, h):
                sc.wait_ge(dx_ready, c * CH + (h + 1))
                if not first(c):
                    sc.wait_ge([k_ready, r_ready, v_ready][i], c * CH)
                nc.scalar.activation(mix[:, i, h, :], dx[:, h, :], ACT.Copy,
                                     scale=par[:, MIX[i], h:h + 1]).then_inc(dx_scaled, 1)

            def norm2(c):
                sc.wait_ge(shift2_ready, c + 1)
                if not first(c):
                    sc.wait_ge(stored, c * 16)
                for q in range(NT):
                    nc.scalar.activation(y[:, q, :], res2[:, q, :], ACT.Identity, bias=shift2[:, q:q + 1],
                                         scale=rstd2[:, q:q + 1]).then_inc(y_ready, 1)

            def reciprocal(c, h):
                sc.wait_ge(den_ready, c * CH + (h + 1))
                if not first(c):
                    sc.wait_ge(rwkv_ready, c * CH)
                nc.scalar.activation(rec[:, h, :], den[:, h, :], ACT.Ln, scale=2.0).then_inc(ln_ready, 1)

            def reciprocal_exp(c, h):
                sc.wait_ge(ln_ready, c * CH + (h + 1))
                nc.scalar.activation(rec[:, h, :], rec[:, h, :], ACT.Exp, scale=-1.0).then_inc(rec_ready, 1)

            def receptance(c, h):
                sc.wait_ge(r_ready, c * CH + (h + 1))
                if not first(c):
                    sc.wait_ge(gated, c * CH)
                nc.scalar.activation(recv[:, h, :], bank_c[:, h, :], ACT.Tanh, scale=0.5).then_inc(recv_ready, 1)

            def rstd(c, mv, lnv, rs, mv_ready, lnv_ready, rstd_ready):
                sc.wait_ge(mv_ready, c * NT + NT)
                nc.scalar.activation(lnv[:, :], mv[:, :, 1], ACT.Ln, bias=eps[:, 0:1]).then_inc(lnv_ready, 1)
                sc.wait_ge(lnv_ready, c + 1)
                nc.scalar.activation(rs[:, :], lnv[:, :], ACT.Exp, scale=-0.5).then_inc(rstd_ready, 1)

            def x1_high(c, h):
                sc.wait_ge(x1T_ready, c * CH + (h + 1))
                if not first(c):
                    sc.wait_ge(up_ready, c * NM)
                nc.scalar.activation(x1hi[:, h, :], bank_a[:, h, :], ACT.Copy).then_inc(x1hi_ready, 1)

            def silu(c, m):
                sc.wait_ge(gate_ready, c * NM + (m + 1))
                if not (first(c) and m < 2):
                    sc.wait_ge(hid_ready, c * NM + (m - 1))
                nc.scalar.activation(act[:, m % 2, :], bank_a[:, m % 2, :], ACT.Silu,
                                     scale=SCALE).then_inc(act_ready, 1)

            def hid_high(c, m):
                sc.wait_ge(hid_ready, c * NM + (m + 1))
                if not first(c):
                    sc.wait_ge(ffn_ready, c * 2)
                nc.scalar.activation(hhi[:, m, :], hid[:, m % NH, :], ACT.Copy).then_inc(hhi_ready, 1)

            def round_(j, ffn, nxt):
                sc.preload_act_table_set("silu_and_others")
                for m in range(NM):
                    if ffn:
                        silu(j - 1, m)
                    if m < CH:
                        receptance(j, m)
                    if nxt:
                        scale_dx(j + 1, m // CH, m % CH)
                    if ffn and m > 0:
                        hid_high(j - 1, m - 1)
                if ffn:
                    hid_high(j - 1, NM - 1)
                sc.preload_act_table_set("natural_log_exp_and_others")
                reciprocal(j, 0)
                reciprocal(j, 1)
                reciprocal_exp(j, 0)
                reciprocal_exp(j, 1)
                if ffn:
                    rstd(j - 1, mv2, lnv2, rstd2, mv2_ready, lnv2_ready, rstd2_ready)
                rstd(j, mv1, lnv1, rstd1, mv1_ready, lnv1_ready, rstd1_ready)
                if nxt:
                    weights(j + 1, 0)
                x1_high(j, 0)
                x1_high(j, 1)
                if ffn:
                    norm2(j - 1)
                if nxt:
                    weights(j + 1, 1)

            def weights(c, h):
                for i in range(4):
                    weight(c, i, h)

            sc.preload_act_table_set("natural_log_exp_and_others")
            sc.wait_ge(par_in, 16)
            nc.scalar.activation(decay[:, :], par[:, DECAY, :], ACT.Exp).then_inc(decay_exp, 1)
            for i in range(3):
                for h in range(CH):
                    scale_dx(0, i, h)
            sc.wait_ge(ffn_in, 48)
            for w_int, w_exact in ((wg_i, wg_r), (wu_i, wu_r), (wd_i, wd_r)):
                nc.scalar.activation(w_exact[:, :, :], w_int[:, :, :], ACT.Copy).then_inc(ffn_w_ready, 1)
            weights(0, 0)
            weights(0, 1)
            round_(0, False, True)
            round_(1, True, True)
            with sc.Fori(2, NC - 1) as j:
                round_(j, True, True)
            round_(NC - 1, True, False)
            sc.preload_act_table_set("silu_and_others")
            for m in range(NM):
                silu(NC - 1, m)
                if m > 0:
                    hid_high(NC - 1, m - 1)
            hid_high(NC - 1, NM - 1)
            sc.preload_act_table_set("natural_log_exp_and_others")
            rstd(NC - 1, mv2, lnv2, rstd2, mv2_ready, lnv2_ready, rstd2_ready)
            norm2(NC - 1)

        @block.vector
        def _(dve):
            def carry_max(c):
                if first(c):
                    return
                nc.vector.tensor_copy(pmax[:, :, 0:1], pmax[:, :, N:N + 1]).then_inc(pmax_carried, 1)

            def running_max(c, h):
                dve.wait_ge(k_ready, c * CH + (h + 1))
                if not first(c):
                    dve.wait_ge(pmax_carried, c)
                nc.vector.tensor_tensor_scan(pmax[:, h, 1:N + 1], neg_decay[:, h:h + 1].broadcast_to([P, N]),
                                             bank_b[:, h, :], pmax[:, h, 0:1], ALU.add,
                                             ALU.max).then_inc(pmax_ready, 1)

            def gaps(c, h):
                dve.wait_ge(pmax_ready, c * CH + (h + 1))
                nc.vector.tensor_tensor(gap[:, h, :], bank_b[:, h, :], pmax[:, h, 0:N],
                                        ALU.subtract).then_inc(gap_ready, 1)

            def exp_args(c, h):
                dve.wait_ge(gap_ready, c * CH + (h + 1))
                for i, s, op in ((IN_NEW, decay[:, h:h + 1], ALU.min), (IN_OLD, decay[:, h:h + 1], ALU.max),
                                 (OUT_OLD, par[:, FIRST, h:h + 1], ALU.max),
                                 (OUT_NEW, par[:, FIRST, h:h + 1], ALU.min)):
                    nc.vector.tensor_scalar(wts[:, i, h, :], gap[:, h, :], s, 0.0, ALU.add,
                                            op).then_inc(args_ready, 1)

            def weights_there(c, h):
                dve.wait_ge(wts_ready, c * (4 * CH) + (4 * h + 4))

            def carry_state(c):
                if first(c):
                    return
                nc.vector.tensor_copy(state[:, :, :, 0:1], state[:, :, :, N:N + 1]).then_inc(state_carried, 1)

            def scan_bb(c, h):
                weights_there(c, h)
                if not first(c):
                    dve.wait_ge(state_carried, c)
                nc.vector.tensor_tensor_scan(state[:, 1, h, 1:N + 1], wts[:, IN_OLD, h, :], wts[:, IN_NEW, h, :],
                                             state[:, 1, h, 0:1], ALU.mult, ALU.add).then_inc(bb_ready, 1)

            def new_kv(c, h):
                dve.wait_ge(v_ready, c * CH + (h + 1))
                nc.vector.tensor_tensor(kv[:, h, :], wts[:, IN_NEW, h, :], bank_d[:, h, :],
                                        ALU.mult).then_inc(kv_ready, 1)

            def scan_aa(c, h):
                dve.wait_ge(kv_ready, c * CH + (h + 1))
                nc.vector.tensor_tensor_scan(state[:, 0, h, 1:N + 1], wts[:, IN_OLD, h, :], kv[:, h, :],
                                             state[:, 0, h, 0:1], ALU.mult, ALU.add).then_inc(aa_ready, 1)

            def den_old(c, h):
                dve.wait_ge(bb_ready, c * CH + (h + 1))
                if not first(c):
                    dve.wait_ge(ln_ready, c * CH)
                nc.vector.tensor_tensor(den[:, h, :], wts[:, OUT_OLD, h, :], state[:, 1, h, 0:N],
                                        ALU.mult).then_inc(den_part, 1)

            def den_sum(c, h):
                dve.wait_ge(den_part, c * CH + (h + 1))
                nc.vector.tensor_tensor(den[:, h, :], den[:, h, :], wts[:, OUT_NEW, h, :],
                                        ALU.add).then_inc(den_ready, 1)

            def num_old(c, h):
                dve.wait_ge(aa_ready, c * CH + (h + 1))
                nc.vector.tensor_tensor(num[:, h, :], wts[:, OUT_OLD, h, :], state[:, 0, h, 0:N], ALU.mult)

            def num_new(c, h):
                nc.vector.tensor_tensor(num2[:, h, :], wts[:, OUT_NEW, h, :], bank_d[:, h, :],
                                        ALU.mult).then_inc(num_parts, 1)

            def gate_num(c, h):
                dve.wait_ge(num_ready, c * CH + (h + 1))
                dve.wait_ge(recv_ready, c * CH + (h + 1))
                nc.vector.scalar_tensor_tensor(out=num[:, h, :], in0=recv[:, h, :], scalar=1.0, in1=num[:, h, :],
                                               op0=ALU.add, op1=ALU.mult).then_inc(gated, 1)

            def divide(c, h):
                dve.wait_ge(gated, c * CH + (h + 1))
                dve.wait_ge(rec_ready, c * CH + (h + 1))
                if not first(c):
                    dve.wait_ge(attn_ready, c * 2)
                nc.vector.tensor_tensor(rwkv[:, h, :], num[:, h, :], rec[:, h, :],
                                        ALU.mult).then_inc(rwkv_ready, 1)

            def row_stats(c, res, stats, res_ready, stats_ready):
                for q in range(NT):
                    if q % 2 == 0:
                        dve.wait_ge(res_ready, c * 2 + (q // 2 + 1))
                    nc.vector.bn_stats(stats[:, q, :], res[:, q, :]).then_inc(stats_ready, 1)

            def mean_var(stats, mv, mv_ready):
                for q in range(NT):
                    nc.vector.bn_aggr(mv[:, q, :], stats[:, q, :]).then_inc(mv_ready, 1)

            def residual1(c):
                dve.wait_ge(xrow_in, c * 16 + 16)
                for b in range(2):
                    dve.wait_ge(attn_ready, c * 2 + (b + 1))
                    nc.vector.tensor_tensor(res1[:, 2 * b:2 * b + 2, :], attn[:, 2 * b:2 * b + 2, :],
                                            xrow[:, 2 * b:2 * b + 2, :], ALU.add).then_inc(res1_ready, 1)

            def norm1(c):
                dve.wait_ge(rstd1_ready, c + 1)
                if not first(c):
                    dve.wait_ge(x1T_ready, c * CH)
                for q in range(NT):
                    nc.vector.tensor_scalar(x1[:, q, :], res1[:, q, :], mv1[:, q, 0:1], rstd1[:, q:q + 1],
                                            ALU.subtract, ALU.mult).then_inc(x1_ready, 1)

            def x1_low(c, h):
                dve.wait_ge(x1hi_ready, c * CH + (h + 1))
                if not first(c):
                    dve.wait_ge(up_ready, c * NM)
                nc.vector.tensor_tensor(x1lo[:, h, :], bank_a[:, h, :], x1hi[:, h, :].bitcast(f32),
                                        ALU.subtract).then_inc(x1lo_ready, 1)

            def product(c, m):
                dve.wait_ge(act_ready, c * NM + (m + 1))
                dve.wait_ge(up_ready, c * NM + (m + 1))
                if not (first(c) and m < NH):
                    dve.wait_ge(hlo_ready, c * NM + (m - NH + 1))
                nc.vector.tensor_tensor(hid[:, m % NH, :], bank_b[:, m % 2, :], act[:, m % 2, :],
                                        ALU.mult).then_inc(hid_ready, 1)

            def residual2(c):
                if not first(c):
                    dve.wait_ge(y_ready, c * NT)
                for b in range(2):
                    dve.wait_ge(ffn_ready, c * 2 + (b + 1))
                    nc.vector.scalar_tensor_tensor(out=res2[:, 2 * b:2 * b + 2, :], in0=ffn[:, 2 * b:2 * b + 2, :],
                                                   scalar=SCALE * SCALE, in1=x1[:, 2 * b:2 * b + 2, :],
                                                   op0=ALU.mult, op1=ALU.add).then_inc(res2_ready, 1)
                row_stats(c, res2, stats2, res2_ready, stats2_ready)

            def shift_rows2(c):
                dve.wait_ge(rstd2_ready, c + 1)
                nc.vector.scalar_tensor_tensor(out=shift2[:, :], in0=mv2[:, :, 0], scalar=-1.0, in1=rstd2[:, :],
                                               op0=ALU.mult, op1=ALU.mult).then_inc(shift2_ready, 1)

            def round_(j, ffn, nxt):
                def hidden(m):
                    if ffn:
                        product(j - 1, m)
                carry_state(j)
                scan_bb(j, 0)
                scan_bb(j, 1)
                new_kv(j, 0)
                hidden(0)
                new_kv(j, 1)
                scan_aa(j, 0)
                hidden(1)
                scan_aa(j, 1)
                den_old(j, 0)
                hidden(2)
                den_old(j, 1)
                num_old(j, 0)
                hidden(3)
                num_old(j, 1)
                num_new(j, 0)
                hidden(4)
                num_new(j, 1)
                den_sum(j, 0)
                hidden(5)
                den_sum(j, 1)
                gate_num(j, 0)
                gate_num(j, 1)
                divide(j, 0)
                divide(j, 1)
                if ffn:
                    residual2(j - 1)
                    dve.wait_ge(stats2_ready, (j - 1) * NT + NT)
                residual1(j)
                if ffn:
                    mean_var(stats2, mv2, mv2_ready)
                row_stats(j, res1, stats1, res1_ready, stats1_ready)
                dve.wait_ge(stats1_ready, j * NT + NT)
                if nxt:
                    carry_max(j + 1)
                mean_var(stats1, mv1, mv1_ready)
                if nxt:
                    running_max(j + 1, 0)
                if ffn:
                    shift_rows2(j - 1)
                norm1(j)
                if nxt:
                    running_max(j + 1, 1)
                    gaps(j + 1, 0)
                    gaps(j + 1, 1)
                    exp_args(j + 1, 0)
                x1_low(j, 0)
                x1_low(j, 1)
                if nxt:
                    exp_args(j + 1, 1)

            nc.vector.memset(eps[:, :], EPS)
            nc.vector.memset(pmax[:, :, 0:1], START)
            nc.vector.memset(state[:, :, :, 0:1], 0.0).then_inc(consts_ready, 1)
            dve.wait_ge(decay_exp, 1)
            nc.vector.tensor_scalar(neg_decay[:, :], decay[:, :], -1.0, None, ALU.mult).then_inc(decay_ready, 1)
            dve.wait_ge(consts_ready, 1)
            dve.wait_ge(decay_ready, 1)
            running_max(0, 0)
            running_max(0, 1)
            gaps(0, 0)
            gaps(0, 1)
            exp_args(0, 0)
            exp_args(0, 1)
            round_(0, False, True)
            round_(1, True, True)
            with dve.Fori(2, NC - 1) as j:
                round_(j, True, True)
            round_(NC - 1, True, False)
            for m in range(NM):
                product(NC - 1, m)
            residual2(NC - 1)
            dve.wait_ge(stats2_ready, NC * NT)
            mean_var(stats2, mv2, mv2_ready)
            shift_rows2(NC - 1)

        @block.tensor
        def _(pe):
            def project(c, i):
                w, bank, ready = ((wkT, bank_b, k_ready), (wrT, bank_c, r_ready), (wvT, bank_d, v_ready))[i]
                pe.wait_ge(mixed, c * (3 * CH) + (i + 1) * CH)
                if not first(c):
                    if i == 0:
                        if not (isinstance(c, int) and c < 2):
                            pe.wait_ge(hid_ready, (c - 1) * NM)
                        pe.wait_ge(gap_ready, c * CH)
                    elif i == 1:
                        if not (isinstance(c, int) and c < 2):
                            pe.wait_ge(res2_ready, (c - 1) * 2)
                        pe.wait_ge(recv_ready, c * CH)
                    else:
                        pe.wait_ge(num_parts, c * CH)
                for d in range(CH):
                    for h in range(CH):
                        mm = nc.tensor.matmul(bank[:, d, :], w[:, h, d * P:(d + 1) * P], mix[:, i, h, :],
                                              start=(h == 0), stop=(h == CH - 1))
                    mm.then_inc(ready, 1)

            def attention_out(c):
                pe.wait_ge(rwkv_ready, c * CH + CH)
                if not first(c):
                    pe.wait_ge(act_ready, c * NM)
                for q in range(NT):
                    for h in range(CH):
                        mm = nc.tensor.matmul(attn[:, q, :], rwkv[:, h, q * P:(q + 1) * P], woT[:, h, :],
                                              start=(h == 0), stop=(h == CH - 1))
                    if q % 2 == 1:
                        mm.then_inc(attn_ready, 1)

            def transpose_x1(c):
                pe.wait_ge(x1_ready, c * NT + NT)
                for h in range(CH):
                    for q in range(NT):
                        mm = nc.tensor.transpose(bank_a[:, h, q * P:(q + 1) * P], x1[:, q, h * P:(h + 1) * P],
                                                 ident[:, :])
                    mm.then_inc(x1T_ready, 1)

            def gate_up(c):
                pe.wait_ge(x1lo_ready, c * CH + CH)
                if first(c):
                    pe.wait_ge(gap_ready, 2 * CH)
                elif not (isinstance(c, int) and c == NC - 1):
                    pe.wait_ge(gap_ready, c * CH + 2 * CH)
                for m in range(NM):
                    for w, bank, ready in ((wg_r, bank_a, gate_ready), (wu_r, bank_b, up_ready)):
                        if not (first(c) and m < 2):
                            pe.wait_ge(act_ready if bank is bank_a else hid_ready, c * NM + (m - 1))
                        for h in range(CH):
                            for part in (x1hi, x1lo):
                                mm = nc.tensor.matmul(bank[:, m % 2, :], w[:, h, m * P:(m + 1) * P], part[:, h, :],
                                                      start=(h == 0 and part is x1hi),
                                                      stop=(h == CH - 1 and part is x1lo))
                        mm.then_inc(ready, 1)

            def down(c, last=False):
                if not last:
                    pe.wait_ge(recv_ready, c * CH + 2 * CH)
                for m in range(NM):
                    pe.wait_ge(hhi_ready, c * NM + (m + 1))
                    pe.wait_ge(hlo_ready, c * NM + (m + 1))
                    for q in range(NT):
                        for part in (hhi, hlo):
                            mm = nc.tensor.matmul(ffn[:, q, :], part[:, m, q * P:(q + 1) * P], wd_r[:, m, :],
                                                  start=(m == 0 and q % 2 == 0 and part is hhi),
                                                  stop=(m == NM - 1 and part is hlo), skip_group_check=True)
                        if m == NM - 1 and q % 2 == 1:
                            mm.then_inc(ffn_ready, 1)

            def round_(j, ffn, nxt):
                if ffn:
                    gate_up(j - 1)
                    down(j - 1)
                attention_out(j)
                if nxt:
                    project(j + 1, 0)
                    project(j + 1, 1)
                transpose_x1(j)
                if nxt:
                    project(j + 1, 2)

            pe.wait_ge(proj_in, 48)
            project(0, 0)
            project(0, 1)
            project(0, 2)
            pe.wait_ge(wo_in, 16)
            pe.wait_ge(ident_ready, 1)
            round_(0, False, True)
            pe.wait_ge(ffn_w_ready, 3)
            round_(1, True, True)
            with pe.Fori(2, NC - 1) as j:
                round_(j, True, True)
            round_(NC - 1, True, False)
            gate_up(NC - 1)
            down(NC - 1, last=True)


def kernel(**inputs):
    import numpy as np
    import concourse.bacc as bacc
    from concourse.bass_utils import run_bass_kernel_spmd

    a = {k[3:]: np.asarray(v) for k, v in inputs.items()}
    x = a["attn_x"][0]
    xT = np.zeros((x.shape[1], x.shape[0] + 1), x.dtype)
    xT[:, 1:] = x.T
    arrays = {
        "xT": xT,
        "x": x,
        "params": np.stack([a["attn_time_decay"], a["attn_time_first"], a["attn_time_mix_k"].reshape(-1),
                            a["attn_time_mix_r"].reshape(-1), a["attn_time_mix_v"].reshape(-1)])
                  .reshape(5, -1, 128).transpose(2, 0, 1),
        "wk": a["attn_Wk"].T, "wv": a["attn_Wv"].T, "wr": a["attn_Wr"].T, "wo": a["attn_Wo"].T,
        "wg": a["ffn_w_gate"].T, "wu": a["ffn_w_up"].T, "wd": a["ffn_w_down"].T,
    }
    arrays = {k: np.ascontiguousarray(v) for k, v in arrays.items()}
    nc = bacc.Bacc("TRN2", target_bir_lowering=False, num_devices=1)
    args = [nc.dram_tensor(k, v.shape, mybir.dt.from_np(v.dtype), kind="ExternalInput").ap()
            for k, v in arrays.items()]
    out = nc.dram_tensor("out", x.shape, mybir.dt.float32, kind="ExternalOutput").ap()
    rwkv_swiglu_kernel(nc, *args, out)
    r = run_bass_kernel_spmd(nc, [arrays], core_ids=[0])
    return np.asarray(r.results[0]["out"]).reshape(1, *x.shape)
```

```python
import concourse.bass as bass
from concourse import mybir
from contextlib import ExitStack


def rwkv_swiglu_kernel(nc: bass.Bass, xT: bass.AP, x: bass.AP, params: bass.AP, wk: bass.AP, wv: bass.AP,
                       wr: bass.AP, wo: bass.AP, wg: bass.AP, wu: bass.AP, wd: bass.AP, out: bass.AP):
    f32 = mybir.dt.float32
    f32r = mybir.dt.float32r
    i32 = mybir.dt.int32
    ALU = mybir.AluOpType
    ACT = mybir.ActivationFunctionType

    P = 128
    T, C = x.shape
    H = wd.shape[0]
    N = 512
    NC = T // N
    CH = C // P
    NT = N // P
    NM = H // P
    NH = 3
    SCALE = 1.0 / 127.0
    EPS = 1e-5
    START = -1e38
    DECAY, FIRST, MIX = 0, 1, 2
    K, V, R = range(3)
    IN_NEW, IN_OLD, OUT_OLD, OUT_NEW = range(4)

    xT_v = xT.rearrange("(h p) t -> p h t", p=P)
    x_v = x.rearrange("(n p) c -> p n c", p=P)
    out_v = out.rearrange("(n p) c -> p n c", p=P)

    ctx = ExitStack()
    with ctx:
        def sb(name, shape, dt=f32):
            return ctx.enter_context(nc.sbuf_tensor(name, shape, dt))

        def ps(name, shape):
            return ctx.enter_context(nc.psum_tensor(name, shape, f32))

        def sem(name):
            return ctx.enter_context(nc.semaphore(name))

        xt = sb("xt", [P, CH, N + 1])
        xrow = sb("xrow", [P, NT, C])
        par = sb("par", [P, 5, CH])
        decay = sb("decay", [P, CH])
        neg_decay = sb("neg_decay", [P, CH])
        eps = sb("eps", [P, 1])
        wkT = sb("wkT", [P, CH, C])
        wrT = sb("wrT", [P, CH, C])
        wvT = sb("wvT", [P, CH, C])
        woT = sb("woT", [P, CH, C])
        wg_i = sb("wg_i", [P, CH, H], i32)
        wu_i = sb("wu_i", [P, CH, H], i32)
        wd_i = sb("wd_i", [P, NM, C], i32)
        wg_r = sb("wg_r", [P, CH, H], f32r)
        wu_r = sb("wu_r", [P, CH, H], f32r)
        wd_r = sb("wd_r", [P, NM, C], f32r)
        ident = sb("ident", [P, P])
        dx = sb("dx", [P, CH, N])
        mix = sb("mix", [P, 3, CH, N])
        pmax = sb("pmax", [P, CH, N + 1])
        state = sb("state", [P, 2, CH, N + 1])
        gap = sb("gap", [P, CH, N])
        wts = sb("wts", [P, 4, CH, N])
        kv = sb("kv", [P, CH, N])
        num = sb("num", [P, CH, N])
        num2 = sb("num2", [P, CH, N])
        den = sb("den", [P, CH, N])
        rec = sb("rec", [P, CH, N])
        recv = sb("recv", [P, CH, N])
        rwkv = sb("rwkv", [P, CH, N])
        res1 = sb("res1", [P, NT, C])
        stats1 = sb("stats1", [P, NT, 6])
        mv1 = sb("mv1", [P, NT, 2])
        lnv1 = sb("lnv1", [P, NT])
        rstd1 = sb("rstd1", [P, NT])
        shift1 = sb("shift1", [P, NT])
        x1 = sb("x1", [P, NT, C])
        x1hi = sb("x1hi", [P, CH, N], f32r)
        x1lo = sb("x1lo", [P, CH, N], f32r)
        act = sb("act", [P, 2, N])
        hid = sb("hid", [P, NH, N])
        hhi = sb("hhi", [P, NM, N], f32r)
        hlo = sb("hlo", [P, NM, N], f32r)
        res2 = sb("res2", [P, NT, C])
        stats2 = sb("stats2", [P, NT, 6])
        mv2 = sb("mv2", [P, NT, 2])
        lnv2 = sb("lnv2", [P, NT])
        rstd2 = sb("rstd2", [P, NT])
        shift2 = sb("shift2", [P, NT])
        y = sb("y", [P, NT, C])

        bank_a = ps("bank_a", [P, 2, N])
        bank_b = ps("bank_b", [P, 2, N])
        bank_c = ps("bank_c", [P, 2, N])
        bank_d = ps("bank_d", [P, 2, N])
        attn = bank_b[:, :, :].rearrange("p b (n c) -> p (b n) c", c=C)
        ffn = bank_a[:, :, :].rearrange("p b (n c) -> p (b n) c", c=C)

        par_in = sem("par_in")
        proj_in = sem("proj_in")
        wo_in = sem("wo_in")
        ffn_in = sem("ffn_in")
        xt_in = sem("xt_in")
        xrow_in = sem("xrow_in")
        stored = sem("stored")
        decay_exp = sem("decay_exp")
        decay_ready = sem("decay_ready")
        consts_ready = sem("consts_ready")
        ident_zero = sem("ident_zero")
        ident_ready = sem("ident_ready")
        state_zero = sem("state_zero")
        ffn_w_ready = sem("ffn_w_ready")
        dx_ready = sem("dx_ready")
        dx_scaled = sem("dx_scaled")
        mixed = sem("mixed")
        k_ready = sem("k_ready")
        r_ready = sem("r_ready")
        v_ready = sem("v_ready")
        pmax_carried = sem("pmax_carried")
        pmax_ready = sem("pmax_ready")
        gap_ready = sem("gap_ready")
        args_ready = sem("args_ready")
        wts_ready = sem("wts_ready")
        state_carried = sem("state_carried")
        bb_ready = sem("bb_ready")
        kv_ready = sem("kv_ready")
        aa_ready = sem("aa_ready")
        den_part = sem("den_part")
        den_ready = sem("den_ready")
        num_parts = sem("num_parts")
        num_ready = sem("num_ready")
        ln_ready = sem("ln_ready")
        rec_ready = sem("rec_ready")
        recv_ready = sem("recv_ready")
        gated = sem("gated")
        rwkv_ready = sem("rwkv_ready")
        attn_ready = sem("attn_ready")
        res1_ready = sem("res1_ready")
        stats1_ready = sem("stats1_ready")
        mv1_ready = sem("mv1_ready")
        lnv1_ready = sem("lnv1_ready")
        rstd1_ready = sem("rstd1_ready")
        shift1_ready = sem("shift1_ready")
        x1_ready = sem("x1_ready")
        x1T_ready = sem("x1T_ready")
        x1hi_ready = sem("x1hi_ready")
        x1lo_ready = sem("x1lo_ready")
        gate_ready = sem("gate_ready")
        up_ready = sem("up_ready")
        act_ready = sem("act_ready")
        hid_ready = sem("hid_ready")
        hhi_ready = sem("hhi_ready")
        hlo_ready = sem("hlo_ready")
        hlo_last_ready = sem("hlo_last_ready")
        ffn_ready = sem("ffn_ready")
        res2_ready = sem("res2_ready")
        stats2_ready = sem("stats2_ready")
        mv2_ready = sem("mv2_ready")
        lnv2_ready = sem("lnv2_ready")
        rstd2_ready = sem("rstd2_ready")
        shift2_ready = sem("shift2_ready")
        y_ready = sem("y_ready")

        block = ctx.enter_context(nc.Block())

        def first(c):
            return isinstance(c, int) and c == 0

        @block.sync
        def _(sp):
            def load_xt(c):
                if not first(c):
                    sp.wait_ge(mixed, c * (3 * CH))
                sp.dma_start(xt[:, :, :], xT_v[:, :, bass.ds(c * N, N + 1)]).then_inc(xt_in, 16)

            def load_xrow(c):
                if not first(c):
                    sp.wait_ge(res1_ready, c * 2)
                sp.dma_start(xrow[:, :, :], x_v[:, bass.ds(c * NT, NT), :]).then_inc(xrow_in, 16)

            def store(c):
                sp.wait_ge(y_ready, c * NT + NT)
                sp.dma_start(out_v[:, bass.ds(c * NT, NT), :], y[:, :, :]).then_inc(stored, 16)

            load_xt(0)
            sp.dma_start(wkT[:, :, :], wk.rearrange("(h p) d -> p h d", p=P)).then_inc(proj_in, 16)
            sp.dma_start(wrT[:, :, :], wr.rearrange("(h p) d -> p h d", p=P)).then_inc(proj_in, 16)
            sp.dma_start(wvT[:, :, :], wv.rearrange("(h p) d -> p h d", p=P)).then_inc(proj_in, 16)
            load_xrow(0)
            sp.dma_start(woT[:, :, :], wo.rearrange("(h p) d -> p h d", p=P)).then_inc(wo_in, 16)
            load_xt(1)
            load_xt(2)
            load_xrow(1)
            with sp.Fori(3, NC) as c:
                load_xt(c)
                load_xrow(c - 1)
                store(c - 3)
            load_xrow(NC - 1)
            store(NC - 3)
            store(NC - 2)
            store(NC - 1)
            sp.wait_ge(stored, 16 * NC)

        @block.gpsimd
        def _(pool):
            def diff(c, h):
                if h == 0:
                    pool.wait_ge(xt_in, c * 16 + 16)
                nc.gpsimd.tensor_tensor(dx[:, h, :], xt[:, h, 1:N + 1], xt[:, h, 0:N],
                                        ALU.subtract).then_inc(dx_ready, 1)

            def mixing(c, i, h):
                pool.wait_ge(dx_scaled, (c - 1) * (3 * CH) + (i * CH + h + 1))
                nc.gpsimd.tensor_tensor(mix[:, i, h, :], mix[:, i, h, :], xt[:, h, 0:N],
                                        ALU.add).then_inc(mixed, 1)

            def numerator(c, h):
                pool.wait_ge(num_parts, c * CH + (h + 1))
                nc.gpsimd.tensor_tensor(num[:, h, :], num[:, h, :], num2[:, h, :],
                                        ALU.add).then_inc(num_ready, 1)

            def low_part(c, m):
                pool.wait_ge(hhi_ready, c * NM + (m + 1))
                if not first(c):
                    pool.wait_ge(ffn_ready, c * 2)
                nc.gpsimd.tensor_tensor(hlo[:, m, :], hid[:, m % NH, :], hhi[:, m, :].bitcast(f32),
                                        ALU.subtract).then_inc(hlo_ready, 1)

            def mix_chunk(c):
                diff(c, 0)
                diff(c, 1)
                for i in range(3):
                    for h in range(CH):
                        mixing(c, i, h)

            def round_(j, ffn, nxt):
                if nxt and first(j):
                    mix_chunk(j + 1)
                if ffn:
                    for m in range(4):
                        low_part(j - 1, m)
                numerator(j, 0)
                numerator(j, 1)
                if ffn:
                    low_part(j - 1, 4)
                if nxt and not first(j):
                    mix_chunk(j + 1)

            nc.gpsimd.dma_start(par[:, :, :], params).then_inc(par_in, 16)
            nc.gpsimd.dma_start(wg_i[:, :, :], wg.rearrange("(h p) n -> p h n", p=P)).then_inc(ffn_in, 16)
            nc.gpsimd.dma_start(wu_i[:, :, :], wu.rearrange("(h p) n -> p h n", p=P)).then_inc(ffn_in, 16)
            nc.gpsimd.dma_start(wd_i[:, :, :], wd.rearrange("(m p) c -> p m c", p=P)).then_inc(ffn_in, 16)
            nc.gpsimd.memset(ident[:, :], 0.0).then_inc(ident_zero, 1)
            pool.wait_ge(ident_zero, 1)
            nc.gpsimd.affine_select(out=ident[:, :], in_=ident[:, :], compare_op=ALU.not_equal, fill=1.0, base=0,
                                    pattern=[[-1, P]], channel_multiplier=1).then_inc(ident_ready, 1)
            round_(0, False, True)
            round_(1, True, True)
            with pool.Fori(2, NC - 1) as j:
                round_(j, True, True)
            round_(NC - 1, True, False)
            for m in range(NM - 1):
                low_part(NC - 1, m)

        @block.scalar
        def _(sc):
            def weight(c, i, h):
                sc.wait_ge(args_ready, c * (4 * CH) + (h * 4 + i + 1))
                old = i in (IN_OLD, OUT_OLD)
                nc.scalar.activation(wts[:, i, h, :], wts[:, i, h, :], ACT.Exp,
                                     scale=-1.0 if old else 1.0).then_inc(wts_ready, 1)

            def scale_dx(c, i, h):
                sc.wait_ge(dx_ready, c * CH + (h + 1))
                sc.wait_ge([k_ready, v_ready, r_ready][i], c * CH)
                nc.scalar.activation(mix[:, i, h, :], dx[:, h, :], ACT.Copy,
                                     scale=par[:, MIX + i, h:h + 1]).then_inc(dx_scaled, 1)

            def scale_chunk(c):
                for i in range(3):
                    for h in range(CH):
                        scale_dx(c, i, h)

            def norm1(c):
                sc.wait_ge(shift1_ready, c + 1)
                if not first(c):
                    sc.wait_ge(x1T_ready, c * CH)
                    sc.wait_ge(res2_ready, c * 2)
                for q in range(NT):
                    nc.scalar.activation(x1[:, q, :], res1[:, q, :], ACT.Identity, bias=shift1[:, q:q + 1],
                                         scale=rstd1[:, q:q + 1]).then_inc(x1_ready, 1)

            def norm2(c, rows):
                if 0 in rows:
                    sc.wait_ge(shift2_ready, c + 1)
                    if not first(c):
                        sc.wait_ge(stored, c * 16)
                for q in rows:
                    nc.scalar.activation(y[:, q, :], res2[:, q, :], ACT.Identity, bias=shift2[:, q:q + 1],
                                         scale=rstd2[:, q:q + 1]).then_inc(y_ready, 1)

            def reciprocal(c, h):
                sc.wait_ge(den_ready, c * CH + (h + 1))
                if not first(c):
                    sc.wait_ge(rwkv_ready, c * CH)
                nc.scalar.activation(rec[:, h, :], den[:, h, :], ACT.Ln, scale=2.0).then_inc(ln_ready, 1)

            def reciprocal_exp(c, h):
                sc.wait_ge(ln_ready, c * CH + (h + 1))
                nc.scalar.activation(rec[:, h, :], rec[:, h, :], ACT.Exp, scale=-1.0).then_inc(rec_ready, 1)

            def receptance(c, h):
                sc.wait_ge(r_ready, c * CH + (h + 1))
                if not first(c):
                    sc.wait_ge(gated, c * CH)
                nc.scalar.activation(recv[:, h, :], bank_c[:, h, :], ACT.Tanh, scale=0.5).then_inc(recv_ready, 1)

            def rstd(c, mv, lnv, rs, mv_ready, lnv_ready, rstd_ready):
                sc.wait_ge(mv_ready, c * NT + NT)
                nc.scalar.activation(lnv[:, :], mv[:, :, 1], ACT.Ln, bias=eps[:, 0:1]).then_inc(lnv_ready, 1)
                sc.wait_ge(lnv_ready, c + 1)
                nc.scalar.activation(rs[:, :], lnv[:, :], ACT.Exp, scale=-0.5).then_inc(rstd_ready, 1)

            def x1_high(c, h):
                sc.wait_ge(x1T_ready, c * CH + (h + 1))
                if not first(c):
                    sc.wait_ge(up_ready, c * NM)
                nc.scalar.activation(x1hi[:, h, :], bank_b[:, h, :], ACT.Copy).then_inc(x1hi_ready, 1)

            def silu(c, m):
                sc.wait_ge(gate_ready, c * NM + (m + 1))
                if not (first(c) and m < 2):
                    sc.wait_ge(hid_ready, c * NM + (m - 1))
                nc.scalar.activation(act[:, m % 2, :], bank_a[:, m % 2, :], ACT.Silu,
                                     scale=SCALE).then_inc(act_ready, 1)

            def hid_high(c, m):
                sc.wait_ge(hid_ready, c * NM + (m + 1))
                if not first(c):
                    sc.wait_ge(ffn_ready, c * 2)
                nc.scalar.activation(hhi[:, m, :], hid[:, m % NH, :], ACT.Copy).then_inc(hhi_ready, 1)

            def round_(j, ffn, nxt):
                sc.preload_act_table_set("silu_and_others")
                for m in range(NM):
                    if ffn:
                        silu(j - 1, m)
                    if m == 0:
                        receptance(j, 0)
                    if ffn and m > 0:
                        hid_high(j - 1, m - 1)
                    if m == 3:
                        receptance(j, 1)
                    if ffn and not (isinstance(j, int) and j < 2) and m in (1, 2, 3, 4):
                        norm2(j - 2, [m - 1])
                sc.preload_act_table_set("natural_log_exp_and_others")
                if first(j):
                    scale_chunk(j + 1)
                    exact_ffn_weights()
                reciprocal(j, 0)
                reciprocal_exp(j, 0)
                if ffn:
                    hid_high(j - 1, NM - 1)
                reciprocal(j, 1)
                reciprocal_exp(j, 1)
                if nxt and not first(j):
                    scale_chunk(j + 1)
                if ffn:
                    rstd(j - 1, mv2, lnv2, rstd2, mv2_ready, lnv2_ready, rstd2_ready)
                rstd(j, mv1, lnv1, rstd1, mv1_ready, lnv1_ready, rstd1_ready)
                norm1(j)
                if nxt:
                    weights(j + 1, 0)
                x1_high(j, 0)
                x1_high(j, 1)
                if nxt:
                    weights(j + 1, 1)

            def exact_ffn_weights():
                sc.wait_ge(ffn_in, 48)
                for w_int, w_exact in ((wg_i, wg_r), (wu_i, wu_r), (wd_i, wd_r)):
                    nc.scalar.activation(w_exact[:, :, :], w_int[:, :, :], ACT.Copy).then_inc(ffn_w_ready, 1)

            def weights(c, h):
                for i in range(4):
                    weight(c, i, h)

            sc.preload_act_table_set("natural_log_exp_and_others")
            sc.wait_ge(par_in, 16)
            nc.scalar.activation(decay[:, :], par[:, DECAY, :], ACT.Exp).then_inc(decay_exp, 1)
            weights(0, 0)
            weights(0, 1)
            round_(0, False, True)
            round_(1, True, True)
            with sc.Fori(2, NC - 1) as j:
                round_(j, True, True)
            round_(NC - 1, True, False)
            sc.preload_act_table_set("silu_and_others")
            for m in range(NM):
                silu(NC - 1, m)
                if m > 0:
                    hid_high(NC - 1, m - 1)
                if m == 2:
                    norm2(NC - 2, range(NT))
            hid_high(NC - 1, NM - 1)
            sc.preload_act_table_set("natural_log_exp_and_others")
            rstd(NC - 1, mv2, lnv2, rstd2, mv2_ready, lnv2_ready, rstd2_ready)
            norm2(NC - 1, range(NT))

        @block.vector
        def _(dve):
            def carry_max(c):
                if first(c):
                    return
                nc.vector.tensor_copy(pmax[:, :, 0:1], pmax[:, :, N:N + 1]).then_inc(pmax_carried, 1)

            def running_max(c, h):
                dve.wait_ge(k_ready, c * CH + (h + 1))
                if not first(c):
                    dve.wait_ge(pmax_carried, c)
                nc.vector.tensor_tensor_scan(pmax[:, h, 1:N + 1], neg_decay[:, h:h + 1].broadcast_to([P, N]),
                                             bank_a[:, h, :], pmax[:, h, 0:1], ALU.add,
                                             ALU.max).then_inc(pmax_ready, 1)

            def gaps(c, h):
                dve.wait_ge(pmax_ready, c * CH + (h + 1))
                nc.vector.tensor_tensor(gap[:, h, :], bank_a[:, h, :], pmax[:, h, 0:N],
                                        ALU.subtract).then_inc(gap_ready, 1)

            def exp_args(c, h, which=range(4)):
                dve.wait_ge(gap_ready, c * CH + (h + 1))
                for i in which:
                    s = decay[:, h:h + 1] if i in (IN_NEW, IN_OLD) else par[:, FIRST, h:h + 1]
                    op = ALU.max if i in (IN_OLD, OUT_OLD) else ALU.min
                    nc.vector.tensor_scalar(wts[:, i, h, :], gap[:, h, :], s, 0.0, ALU.add,
                                            op).then_inc(args_ready, 1)

            def weights_there(c, h):
                dve.wait_ge(wts_ready, c * (4 * CH) + (4 * h + 4))

            def carry_state(c):
                if first(c):
                    return
                nc.vector.tensor_copy(state[:, :, :, 0:1], state[:, :, :, N:N + 1]).then_inc(state_carried, 1)

            def scan_bb(c, h):
                weights_there(c, h)
                if not first(c):
                    dve.wait_ge(state_carried, c)
                nc.vector.tensor_tensor_scan(state[:, 1, h, 1:N + 1], wts[:, IN_OLD, h, :], wts[:, IN_NEW, h, :],
                                             state[:, 1, h, 0:1], ALU.mult, ALU.add).then_inc(bb_ready, 1)

            def new_kv(c, h):
                dve.wait_ge(v_ready, c * CH + (h + 1))
                nc.vector.tensor_tensor(kv[:, h, :], wts[:, IN_NEW, h, :], bank_d[:, h, :],
                                        ALU.mult).then_inc(kv_ready, 1)

            def scan_aa(c, h):
                dve.wait_ge(kv_ready, c * CH + (h + 1))
                nc.vector.tensor_tensor_scan(state[:, 0, h, 1:N + 1], wts[:, IN_OLD, h, :], kv[:, h, :],
                                             state[:, 0, h, 0:1], ALU.mult, ALU.add).then_inc(aa_ready, 1)

            def den_old(c, h):
                dve.wait_ge(bb_ready, c * CH + (h + 1))
                if not first(c):
                    dve.wait_ge(ln_ready, c * CH)
                nc.vector.tensor_tensor(den[:, h, :], wts[:, OUT_OLD, h, :], state[:, 1, h, 0:N],
                                        ALU.mult).then_inc(den_part, 1)

            def den_sum(c, h):
                dve.wait_ge(den_part, c * CH + (h + 1))
                nc.vector.tensor_tensor(den[:, h, :], den[:, h, :], wts[:, OUT_NEW, h, :],
                                        ALU.add).then_inc(den_ready, 1)

            def num_old(c, h):
                dve.wait_ge(aa_ready, c * CH + (h + 1))
                nc.vector.tensor_tensor(num[:, h, :], wts[:, OUT_OLD, h, :], state[:, 0, h, 0:N], ALU.mult)

            def num_new(c, h):
                nc.vector.tensor_tensor(num2[:, h, :], wts[:, OUT_NEW, h, :], bank_d[:, h, :],
                                        ALU.mult).then_inc(num_parts, 1)

            def gate_num(c, h):
                dve.wait_ge(num_ready, c * CH + (h + 1))
                dve.wait_ge(recv_ready, c * CH + (h + 1))
                nc.vector.scalar_tensor_tensor(out=num[:, h, :], in0=recv[:, h, :], scalar=1.0, in1=num[:, h, :],
                                               op0=ALU.add, op1=ALU.mult).then_inc(gated, 1)

            def divide(c, h):
                dve.wait_ge(gated, c * CH + (h + 1))
                dve.wait_ge(rec_ready, c * CH + (h + 1))
                if not first(c):
                    dve.wait_ge(attn_ready, c * 2)
                nc.vector.tensor_tensor(rwkv[:, h, :], num[:, h, :], rec[:, h, :],
                                        ALU.mult).then_inc(rwkv_ready, 1)

            def row_stats(c, res, stats, res_ready, stats_ready):
                for q in range(NT):
                    if q % 2 == 0:
                        dve.wait_ge(res_ready, c * 2 + (q // 2 + 1))
                    nc.vector.bn_stats(stats[:, q, :], res[:, q, :]).then_inc(stats_ready, 1)

            def mean_var(stats, mv, mv_ready):
                for q in range(NT):
                    nc.vector.bn_aggr(mv[:, q, :], stats[:, q, :]).then_inc(mv_ready, 1)

            def residual1(c):
                dve.wait_ge(xrow_in, c * 16 + 16)
                if not first(c):
                    dve.wait_ge(x1_ready, c * NT)
                for b in range(2):
                    dve.wait_ge(attn_ready, c * 2 + (b + 1))
                    nc.vector.tensor_tensor(res1[:, 2 * b:2 * b + 2, :], attn[:, 2 * b:2 * b + 2, :],
                                            xrow[:, 2 * b:2 * b + 2, :], ALU.add).then_inc(res1_ready, 1)

            def shift_rows1(c):
                dve.wait_ge(rstd1_ready, c + 1)
                nc.vector.scalar_tensor_tensor(out=shift1[:, :], in0=mv1[:, :, 0], scalar=-1.0, in1=rstd1[:, :],
                                               op0=ALU.mult, op1=ALU.mult).then_inc(shift1_ready, 1)

            def x1_low(c, h):
                dve.wait_ge(x1hi_ready, c * CH + (h + 1))
                if not first(c):
                    dve.wait_ge(up_ready, c * NM)
                nc.vector.tensor_tensor(x1lo[:, h, :], bank_b[:, h, :], x1hi[:, h, :].bitcast(f32),
                                        ALU.subtract).then_inc(x1lo_ready, 1)

            def product(c, m):
                dve.wait_ge(act_ready, c * NM + (m + 1))
                dve.wait_ge(up_ready, c * NM + (m + 1))
                if m >= NH:
                    dve.wait_ge(hlo_ready, c * (NM - 1) + (m - NH + 1))
                elif m < NH - 1 and not first(c):
                    dve.wait_ge(hlo_ready, (c - 1) * (NM - 1) + (m + NM - NH + 1))
                nc.vector.tensor_tensor(hid[:, m % NH, :], bank_b[:, m % 2, :], act[:, m % 2, :],
                                        ALU.mult).then_inc(hid_ready, 1)

            def last_low_part(c):
                dve.wait_ge(hhi_ready, c * NM + NM)
                if not first(c):
                    dve.wait_ge(ffn_ready, c * 2)
                nc.vector.tensor_tensor(hlo[:, NM - 1, :], hid[:, (NM - 1) % NH, :],
                                        hhi[:, NM - 1, :].bitcast(f32), ALU.subtract).then_inc(hlo_last_ready, 1)

            def residual2(c):
                if not first(c):
                    dve.wait_ge(y_ready, c * NT)
                for b in range(2):
                    dve.wait_ge(ffn_ready, c * 2 + (b + 1))
                    nc.vector.scalar_tensor_tensor(out=res2[:, 2 * b:2 * b + 2, :], in0=ffn[:, 2 * b:2 * b + 2, :],
                                                   scalar=SCALE * SCALE, in1=x1[:, 2 * b:2 * b + 2, :],
                                                   op0=ALU.mult, op1=ALU.add).then_inc(res2_ready, 1)
                row_stats(c, res2, stats2, res2_ready, stats2_ready)

            def shift_rows2(c):
                dve.wait_ge(rstd2_ready, c + 1)
                nc.vector.scalar_tensor_tensor(out=shift2[:, :], in0=mv2[:, :, 0], scalar=-1.0, in1=rstd2[:, :],
                                               op0=ALU.mult, op1=ALU.mult).then_inc(shift2_ready, 1)

            def round_(j, ffn, nxt):
                def hidden(m):
                    if ffn:
                        product(j - 1, m)
                carry_state(j)
                scan_bb(j, 0)
                new_kv(j, 0)
                scan_bb(j, 1)
                new_kv(j, 1)
                hidden(0)
                scan_aa(j, 0)
                scan_aa(j, 1)
                hidden(1)
                den_old(j, 0)
                den_old(j, 1)
                hidden(2)
                num_old(j, 0)
                num_old(j, 1)
                hidden(3)
                num_new(j, 0)
                num_new(j, 1)
                hidden(4)
                den_sum(j, 0)
                den_sum(j, 1)
                hidden(5)
                gate_num(j, 0)
                gate_num(j, 1)
                divide(j, 0)
                if ffn:
                    last_low_part(j - 1)
                divide(j, 1)
                if ffn:
                    residual2(j - 1)
                    dve.wait_ge(stats2_ready, (j - 1) * NT + NT)
                residual1(j)
                if ffn:
                    mean_var(stats2, mv2, mv2_ready)
                row_stats(j, res1, stats1, res1_ready, stats1_ready)
                dve.wait_ge(stats1_ready, j * NT + NT)
                if nxt:
                    carry_max(j + 1)
                mean_var(stats1, mv1, mv1_ready)
                if nxt:
                    running_max(j + 1, 0)
                shift_rows1(j)
                if ffn:
                    shift_rows2(j - 1)
                if nxt:
                    running_max(j + 1, 1)
                    gaps(j + 1, 0)
                    gaps(j + 1, 1)
                    exp_args(j + 1, 0)
                    exp_args(j + 1, 1, (IN_NEW, IN_OLD))
                x1_low(j, 0)
                x1_low(j, 1)
                if nxt:
                    exp_args(j + 1, 1, (OUT_OLD, OUT_NEW))

            nc.vector.memset(eps[:, :], EPS)
            nc.vector.memset(pmax[:, :, 0:1], START)
            nc.vector.memset(state[:, :, :, 0:1], 0.0).then_inc(consts_ready, 1)
            dve.wait_ge(xt_in, 16)
            for h in range(CH):
                nc.vector.tensor_tensor(dx[:, h, :], xt[:, h, 1:N + 1], xt[:, h, 0:N],
                                        ALU.subtract).then_inc(dx_ready, 1)
            dve.wait_ge(par_in, 16)
            for i in range(3):
                for h in range(CH):
                    dve.wait_ge(dx_ready, h + 1)
                    nc.vector.scalar_tensor_tensor(out=mix[:, i, h, :], in0=dx[:, h, :],
                                                   scalar=par[:, MIX + i, h:h + 1], in1=xt[:, h, 0:N],
                                                   op0=ALU.mult, op1=ALU.add).then_inc(mixed, 1)
            dve.wait_ge(decay_exp, 1)
            nc.vector.tensor_scalar(neg_decay[:, :], decay[:, :], -1.0, None, ALU.mult).then_inc(decay_ready, 1)
            dve.wait_ge(consts_ready, 1)
            dve.wait_ge(decay_ready, 1)
            running_max(0, 0)
            running_max(0, 1)
            gaps(0, 0)
            gaps(0, 1)
            exp_args(0, 0)
            exp_args(0, 1)
            round_(0, False, True)
            round_(1, True, True)
            with dve.Fori(2, NC - 1) as j:
                round_(j, True, True)
            round_(NC - 1, True, False)
            for m in range(NM):
                product(NC - 1, m)
            last_low_part(NC - 1)
            residual2(NC - 1)
            dve.wait_ge(stats2_ready, NC * NT)
            mean_var(stats2, mv2, mv2_ready)
            shift_rows2(NC - 1)

        @block.tensor
        def _(pe):
            def project(c, i, halves=range(CH)):
                w, bank, ready = ((wkT, bank_a, k_ready), (wvT, bank_d, v_ready), (wrT, bank_c, r_ready))[i]
                pe.wait_ge(mixed, c * (3 * CH) + (i + 1) * CH)
                if not first(c):
                    if i == K:
                        pe.wait_ge(gap_ready, c * CH)
                        if not (isinstance(c, int) and c < 2):
                            pe.wait_ge(res2_ready, (c - 1) * 2)
                    elif i == V:
                        pe.wait_ge(num_parts, c * CH)
                for d in halves:
                    if i == R and not first(c):
                        pe.wait_ge(recv_ready, (c - 1) * CH + (d + 1))
                    for h in range(CH):
                        mm = nc.tensor.matmul(bank[:, d, :], w[:, h, d * P:(d + 1) * P], mix[:, i, h, :],
                                              start=(h == 0), stop=(h == CH - 1))
                    mm.then_inc(ready, 1)

            def attention_out(c):
                pe.wait_ge(rwkv_ready, c * CH + CH)
                if not first(c):
                    pe.wait_ge(hid_ready, c * NM)
                for q in range(NT):
                    for h in range(CH):
                        mm = nc.tensor.matmul(attn[:, q, :], rwkv[:, h, q * P:(q + 1) * P], woT[:, h, :],
                                              start=(h == 0), stop=(h == CH - 1))
                    if q % 2 == 1:
                        mm.then_inc(attn_ready, 1)

            def transpose_x1(c):
                pe.wait_ge(x1_ready, c * NT + NT)
                for h in range(CH):
                    for q in range(NT):
                        mm = nc.tensor.transpose(bank_b[:, h, q * P:(q + 1) * P], x1[:, q, h * P:(h + 1) * P],
                                                 ident[:, :])
                    mm.then_inc(x1T_ready, 1)

            def gate_up(c, tiles):
                if 0 in tiles:
                    if first(c):
                        pe.wait_ge(gap_ready, 2 * CH)
                    elif not (isinstance(c, int) and c == NC - 1):
                        pe.wait_ge(gap_ready, c * CH + 2 * CH)
                for m in tiles:
                    for w, bank, ready in ((wg_r, bank_a, gate_ready), (wu_r, bank_b, up_ready)):
                        if not (first(c) and m < 2):
                            pe.wait_ge(act_ready if bank is bank_a else hid_ready, c * NM + (m - 1))
                        for part, part_ready in ((x1hi, x1hi_ready), (x1lo, x1lo_ready)):
                            for h in range(CH):
                                if m == 0 and bank is bank_a:
                                    pe.wait_ge(part_ready, c * CH + (h + 1))
                                mm = nc.tensor.matmul(bank[:, m % 2, :], w[:, h, m * P:(m + 1) * P], part[:, h, :],
                                                      start=(h == 0 and part is x1hi),
                                                      stop=(h == CH - 1 and part is x1lo))
                        mm.then_inc(ready, 1)

            def down(c):
                pe.wait_ge(act_ready, c * NM + NM)
                for m in range(NM):
                    pe.wait_ge(hhi_ready, c * NM + (m + 1))
                    if m < NM - 1:
                        pe.wait_ge(hlo_ready, c * (NM - 1) + (m + 1))
                    else:
                        pe.wait_ge(hlo_last_ready, c + 1)
                    for q in range(NT):
                        for part in (hhi, hlo):
                            mm = nc.tensor.matmul(ffn[:, q, :], part[:, m, q * P:(q + 1) * P], wd_r[:, m, :],
                                                  start=(m == 0 and q % 2 == 0 and part is hhi),
                                                  stop=(m == NM - 1 and part is hlo), skip_group_check=True)
                        if m == NM - 1 and q % 2 == 1:
                            mm.then_inc(ffn_ready, 1)

            def round_(j, ffn, nxt):
                if ffn:
                    gate_up(j - 1, range(2))
                project(j, R, [1])
                if ffn:
                    gate_up(j - 1, range(2, NM))
                    down(j - 1)
                if nxt and first(j):
                    project(j + 1, K)
                    project(j + 1, V)
                attention_out(j)
                if nxt and not first(j):
                    project(j + 1, K)
                    project(j + 1, V)
                transpose_x1(j)
                if nxt:
                    project(j + 1, R, [0])

            pe.wait_ge(proj_in, 48)
            project(0, K)
            project(0, V)
            project(0, R, [0])
            pe.wait_ge(wo_in, 16)
            pe.wait_ge(ident_ready, 1)
            round_(0, False, True)
            pe.wait_ge(ffn_w_ready, 3)
            round_(1, True, True)
            with pe.Fori(2, NC - 1) as j:
                round_(j, True, True)
            round_(NC - 1, True, False)
            gate_up(NC - 1, range(NM))
            down(NC - 1)


def kernel(**inputs):
    import numpy as np
    import concourse.bacc as bacc
    from concourse.bass_utils import run_bass_kernel_spmd

    a = {k[3:]: np.asarray(v) for k, v in inputs.items()}
    x = a["attn_x"][0]
    xT = np.zeros((x.shape[1], x.shape[0] + 1), x.dtype)
    xT[:, 1:] = x.T
    arrays = {
        "xT": xT,
        "x": x,
        "params": np.stack([a["attn_time_decay"], a["attn_time_first"], a["attn_time_mix_k"].reshape(-1),
                            a["attn_time_mix_v"].reshape(-1), a["attn_time_mix_r"].reshape(-1)])
                  .reshape(5, -1, 128).transpose(2, 0, 1),
        "wk": a["attn_Wk"].T, "wv": a["attn_Wv"].T, "wr": a["attn_Wr"].T, "wo": a["attn_Wo"].T,
        "wg": a["ffn_w_gate"].T, "wu": a["ffn_w_up"].T, "wd": a["ffn_w_down"].T,
    }
    arrays = {k: np.ascontiguousarray(v) for k, v in arrays.items()}
    nc = bacc.Bacc("TRN2", target_bir_lowering=False, num_devices=1)
    args = [nc.dram_tensor(k, v.shape, mybir.dt.from_np(v.dtype), kind="ExternalInput").ap()
            for k, v in arrays.items()]
    out = nc.dram_tensor("out", x.shape, mybir.dt.float32, kind="ExternalOutput").ap()
    rwkv_swiglu_kernel(nc, *args, out)
    r = run_bass_kernel_spmd(nc, [arrays], core_ids=[0])
    return np.asarray(r.results[0]["out"]).reshape(1, *x.shape)
```

```python
import concourse.bass as bass
from concourse import mybir
from contextlib import ExitStack


def rwkv_swiglu_kernel(nc: bass.Bass, xT: bass.AP, x: bass.AP, params: bass.AP, wk: bass.AP, wv: bass.AP,
                       wr: bass.AP, wo: bass.AP, wg: bass.AP, wu: bass.AP, wd: bass.AP, out: bass.AP):
    f32 = mybir.dt.float32
    f32r = mybir.dt.float32r
    i32 = mybir.dt.int32
    ALU = mybir.AluOpType
    ACT = mybir.ActivationFunctionType

    P = 128
    T, C = x.shape
    H = wd.shape[0]
    N = 512
    NC = T // N + 1
    CH = C // P
    NT = N // P
    NM = H // P
    NP = NM - 2
    NH = 3
    SCALE = 1.0 / 127.0
    EPS = 1e-5
    EXACT = 4096.0
    START = -1e38
    DECAY, FIRST, MIX = 0, 1, 2
    K, V, R = range(3)
    IN_NEW, IN_OLD, OUT_OLD, OUT_NEW = range(4)

    xT_v = xT.rearrange("(h p) t -> p h t", p=P)
    x_v = x.rearrange("(n p) c -> p n c", p=P)
    out_v = out.rearrange("(n p) c -> p n c", p=P)

    ctx = ExitStack()
    with ctx:
        def sb(name, shape, dt=f32):
            return ctx.enter_context(nc.sbuf_tensor(name, shape, dt))

        def ps(name, shape):
            return ctx.enter_context(nc.psum_tensor(name, shape, f32))

        def sem(name):
            return ctx.enter_context(nc.semaphore(name))

        xt = sb("xt", [P, CH, N + 1])
        xt0 = sb("xt0", [P, CH, N // 2 + 1])
        xrow = sb("xrow", [P, NT, C])
        par = sb("par", [P, 5, CH])
        decay = sb("decay", [P, CH])
        neg_decay = sb("neg_decay", [P, CH])
        eps = sb("eps", [P, 1])
        wkT = sb("wkT", [P, CH, C])
        wrT = sb("wrT", [P, CH, C])
        wvT = sb("wvT", [P, CH, C])
        woT = sb("woT", [P, CH, C])
        wg_i = sb("wg_i", [P, CH, H], i32)
        wu_i = sb("wu_i", [P, CH, H], i32)
        wd_i = sb("wd_i", [P, NM, C], i32)
        wg_r = sb("wg_r", [P, CH, H], f32r)
        wu_r = sb("wu_r", [P, CH, H], f32r)
        wd_r = sb("wd_r", [P, NM, C], f32r)
        wg_f = wg_i[:, :, :].bitcast(f32)
        wu_f = wu_i[:, :, :].bitcast(f32)
        wd_f = wd_i[:, :, :].bitcast(f32)
        squares = sb("squares", [P, 6])
        squares_max = sb("squares_max", [P, 1])
        out_of_range = sb("out_of_range", [P, 1])
        ones = sb("ones", [P, 1])
        zeros = sb("zeros", [P, C])
        wide = sb("wide", [1, 1], i32)
        ident = sb("ident", [P, P])
        dx = sb("dx", [P, CH, N])
        mix = sb("mix", [P, 3, CH, N])
        pmax = sb("pmax", [P, CH, N + 1])
        state = sb("state", [P, 2, CH, N + 1])
        gap = sb("gap", [P, CH, N])
        wts = sb("wts", [P, 4, CH, N])
        kv = sb("kv", [P, CH, N])
        num = sb("num", [P, CH, N])
        num2 = sb("num2", [P, CH, N])
        den = sb("den", [P, CH, N])
        recv = sb("recv", [P, CH, N])
        rwkv = sb("rwkv", [P, CH, N])
        res1 = sb("res1", [P, NT, C])
        stats1 = sb("stats1", [P, NT, 6])
        mv1 = sb("mv1", [P, NT, 2])
        lnv1 = sb("lnv1", [P, NT])
        rstd1 = sb("rstd1", [P, NT])
        shift1 = sb("shift1", [P, NT])
        x1 = sb("x1", [P, NT, C])
        x1_last = sb("x1_last", [P, NT // 2, C])
        res2_last = sb("res2_last", [P, NT // 2, C])
        y_last = sb("y_last", [P, NT // 2, C])
        x1hi = sb("x1hi", [P, CH, N], f32r)
        x1lo = sb("x1lo", [P, CH, N], f32r)
        act = sb("act", [P, 2, N])
        hid = sb("hid", [P, NH, N])
        dx0 = act[:, 0, :].rearrange("p (h n) -> p h n", h=CH)
        mix0 = hid[:, :, :].rearrange("p i (h n) -> p i h n", h=CH)
        hhi = sb("hhi", [P, NM, N], f32r)
        hlo = sb("hlo", [P, NM, N], f32r)
        res2 = sb("res2", [P, NT, C])
        stats2 = sb("stats2", [P, NT, 6])
        mv2 = sb("mv2", [P, NT, 2])
        lnv2 = sb("lnv2", [P, NT])
        rstd2 = sb("rstd2", [P, NT])
        shift2 = sb("shift2", [P, NT])
        y = sb("y", [P, NT, C])

        bank_a = ps("bank_a", [P, 2, N])
        bank_b = ps("bank_b", [P, 2, N])
        bank_c = ps("bank_c", [P, 2, N])
        bank_d = ps("bank_d", [P, 2, N])
        attn = bank_b[:, :, :].rearrange("p b (n c) -> p (b n) c", c=C)
        ffn = bank_a[:, :, :].rearrange("p b (n c) -> p (b n) c", c=C)

        par_in = sem("par_in")
        wk_in = sem("wk_in")
        wv_in = sem("wv_in")
        wr_in = sem("wr_in")
        wo_in = sem("wo_in")
        wg_in = sem("wg_in")
        wu_in = sem("wu_in")
        wd_in = sem("wd_in")
        xt0_in = sem("xt0_in")
        xt_in = sem("xt_in")
        xrow_in = sem("xrow_in")
        stored = sem("stored")
        decay_exp = sem("decay_exp")
        decay_ready = sem("decay_ready")
        consts_ready = sem("consts_ready")
        zeros_ready = sem("zeros_ready")
        ident_zero = sem("ident_zero")
        ident_ready = sem("ident_ready")
        state_zero = sem("state_zero")
        wg_ready = sem("wg_ready")
        wu_ready = sem("wu_ready")
        wd_ready = sem("wd_ready")
        ffn_w_f32_ready = sem("ffn_w_f32_ready")
        squares_ready = sem("squares_ready")
        squares_max_ready = sem("squares_max_ready")
        out_of_range_ready = sem("out_of_range_ready")
        out_of_range_total = sem("out_of_range_total")
        wide_ready = sem("wide_ready")
        num_ready_dve = sem("num_ready_dve")
        dx0_ready = sem("dx0_ready")
        kv0_mixed = sem("kv0_mixed")
        r0_scaled = sem("r0_scaled")
        r0_mixed = sem("r0_mixed")
        v2_scaled = sem("v2_scaled")
        v2_mixed = sem("v2_mixed")
        dx_ready = sem("dx_ready")
        dx_scaled = sem("dx_scaled")
        mixed = sem("mixed")
        k_ready = sem("k_ready")
        r_ready = sem("r_ready")
        v_ready = sem("v_ready")
        pmax_carried = sem("pmax_carried")
        pmax_ready = sem("pmax_ready")
        gap_ready = sem("gap_ready")
        args_ready = sem("args_ready")
        wts_ready = sem("wts_ready")
        state_carried = sem("state_carried")
        bb_ready = sem("bb_ready")
        kv_ready = sem("kv_ready")
        aa_ready = sem("aa_ready")
        den_part = sem("den_part")
        den_ready = sem("den_ready")
        num_parts = sem("num_parts")
        num_ready = sem("num_ready")
        ln_ready = sem("ln_ready")
        rec_ready = sem("rec_ready")
        recv_ready = sem("recv_ready")
        gated = sem("gated")
        rwkv_ready = sem("rwkv_ready")
        attn_ready = sem("attn_ready")
        res1_ready = sem("res1_ready")
        stats1_ready = sem("stats1_ready")
        mv1_ready = sem("mv1_ready")
        lnv1_ready = sem("lnv1_ready")
        rstd1_ready = sem("rstd1_ready")
        shift1_ready = sem("shift1_ready")
        x1_ready = sem("x1_ready")
        x1T_ready = sem("x1T_ready")
        x1hi_ready = sem("x1hi_ready")
        x1lo_ready = sem("x1lo_ready")
        gate_ready = sem("gate_ready")
        up_ready = sem("up_ready")
        act_ready = sem("act_ready")
        hid_ready = sem("hid_ready")
        hhi_ready = sem("hhi_ready")
        hlo_ready = sem("hlo_ready")
        hlo_last_ready = sem("hlo_last_ready")
        ffn_ready = sem("ffn_ready")
        res2_ready = sem("res2_ready")
        stats2_ready = sem("stats2_ready")
        mv2_ready = sem("mv2_ready")
        lnv2_ready = sem("lnv2_ready")
        rstd2_ready = sem("rstd2_ready")
        shift2_ready = sem("shift2_ready")
        y_ready = sem("y_ready")
        y_last_ready = sem("y_last_ready")

        block = ctx.enter_context(nc.Block())

        def first(c):
            return isinstance(c, int) and c == 0

        def last(c):
            return isinstance(c, int) and c == NC - 1

        def steps(c):
            return N // 2 if isinstance(c, int) and c in (0, NC - 1) else N

        def start(c):
            return 0 if first(c) else c * N - N // 2

        def x1_of(c):
            return x1_last if last(c) else x1

        def gate_bank(c):
            return bank_c if last(c) else bank_a

        def up_bank(c):
            return bank_d if last(c) else bank_b

        def halved(c):
            return N // steps(c)

        def share(c, i, h):
            return CH + 1 if isinstance(c, int) and (c, i, h) == (2, R, 0) else 1

        @block.sync
        def _(sp):
            def rows(c):
                return bass.ds(0 if first(c) else c * NT - NT // 2, steps(c) // P)

            def load_xt(c):
                if not (isinstance(c, int) and c == 1):
                    sp.wait_ge(mixed, (c - 1) * (3 * CH))
                sp.dma_start(xt[:, :, 0:steps(c) + 1],
                             xT_v[:, :, bass.ds(start(c), steps(c) + 1)]).then_inc(xt_in, 16)

            def load_xrow(c):
                if not first(c):
                    sp.wait_ge(res1_ready, c * 2)
                sp.dma_start(xrow[:, 0:steps(c) // P, :],
                             x_v[:, rows(c), :]).then_inc(xrow_in, 16)

            def store(c):
                sp.wait_ge(y_ready, c * NT + NT)
                sp.dma_start(out_v[:, rows(c), :], y[:, 0:steps(c) // P, :]).then_inc(stored, 16)

            def store_half(c, b):
                sp.wait_ge(y_ready, c * NT + 2 * b + 2)
                sp.dma_start(out_v[:, bass.ds(c * NT - NT // 2 + 2 * b, 2), :],
                             y[:, 2 * b:2 * b + 2, :]).then_inc(stored, 16)

            def store_last():
                c = NC - 1
                sp.wait_ge(y_last_ready, steps(c) // P)
                sp.dma_start(out_v[:, rows(c), :], y_last[:, :, :]).then_inc(stored, 16)

            sp.dma_start(xt0[:, :, :], xT_v[:, :, 0:steps(0) + 1]).then_inc(xt0_in, 16)
            sp.dma_start(wkT[:, :, :], wk.rearrange("(h p) d -> p h d", p=P)).then_inc(wk_in, 16)
            load_xt(1)
            sp.dma_start(wg_i[:, :, :], wg.rearrange("(h p) n -> p h n", p=P)).then_inc(wg_in, 16)
            sp.dma_start(wu_i[:, :, :], wu.rearrange("(h p) n -> p h n", p=P)).then_inc(wu_in, 16)
            sp.dma_start(wd_i[:, :, :], wd.rearrange("(m p) c -> p m c", p=P)).then_inc(wd_in, 16)
            sp.dma_start(woT[:, :, :], wo.rearrange("(h p) d -> p h d", p=P)).then_inc(wo_in, 16)
            load_xrow(0)
            load_xt(2)
            load_xrow(1)

            def loads_and_store(c):
                load_xt(c)
                load_xrow(c - 1)
                store(c - 3)
            loads_and_store(3)
            with sp.Fori(4, NC - 1) as c:
                loads_and_store(c)
            loads_and_store(NC - 1)
            load_xrow(NC - 1)
            store(NC - 3)
            store_half(NC - 2, 0)
            store_half(NC - 2, 1)
            store_last()
            sp.wait_ge(stored, 16 * (NC + 1))

        @block.gpsimd
        def _(pool):
            def diff(c, h):
                if h == 0:
                    pool.wait_ge(xt_in, c * 16)
                n = steps(c)
                nc.gpsimd.tensor_tensor(dx[:, h, 0:n], xt[:, h, 1:n + 1], xt[:, h, 0:n],
                                        ALU.subtract).then_inc(dx_ready, 1)

            def mixing(c, i, h):
                pool.wait_ge(dx_scaled, (c - 1) * (3 * CH) + (i * CH + h + 1))
                n = steps(c)
                nc.gpsimd.tensor_tensor(mix[:, i, h, 0:n], mix[:, i, h, 0:n], xt[:, h, 0:n],
                                        ALU.add).then_inc(mixed, share(c, i, h))

            def numerator(c, h):
                pool.wait_ge(num_parts, c * CH + (h + 1))
                n = steps(c)
                nc.gpsimd.tensor_tensor(num[:, h, 0:n], num[:, h, 0:n], num2[:, h, 0:n],
                                        ALU.add).then_inc(num_ready, 1)

            def low_part(c, m):
                pool.wait_ge(hhi_ready, c * NM + (m + 1))
                if not first(c):
                    pool.wait_ge(ffn_ready, c * 2)
                n = steps(c)
                nc.gpsimd.tensor_tensor(hlo[:, m, 0:n], hid[:, m % NH, 0:n], hhi[:, m, 0:n].bitcast(f32),
                                        ALU.subtract).then_inc(hlo_ready, 1)

            def mix_v2():
                pool.wait_ge(dx_scaled, 3 * CH)
                diff(2, 0)
                diff(2, 1)
                pool.wait_ge(v_ready, 2 * CH)
                for h in range(CH):
                    pool.wait_ge(dx_ready, CH + h + 1)
                    nc.gpsimd.tensor_scalar(mix[:, V, h, :], dx[:, h, :], par[:, MIX + V, h:h + 1], None,
                                            ALU.mult).then_inc(v2_scaled, 1)
                    pool.wait_ge(v2_scaled, h + 1)
                    nc.gpsimd.tensor_tensor(mix[:, V, h, :], mix[:, V, h, :], xt[:, h, 0:N],
                                            ALU.add).then_inc(v2_mixed, 1)

            def mix_chunk(c, which=range(3)):
                if not (isinstance(c, int) and c == 2):
                    diff(c, 0)
                    diff(c, 1)
                for i in which:
                    for h in range(CH):
                        mixing(c, i, h)

            def round_(j, ffn, nxt):
                if ffn:
                    for m in range(NP - 1):
                        low_part(j - 1, m)
                if not last(j):
                    numerator(j, 0)
                if ffn:
                    low_part(j - 1, NP - 1)
                if not last(j):
                    numerator(j, 1)
                if nxt:
                    mix_chunk(j + 1, (K, R) if isinstance(j, int) and j == 1 else range(3))

            nc.gpsimd.memset(ident[:, :], 0.0).then_inc(ident_zero, 1)
            pool.wait_ge(ident_zero, 1)
            nc.gpsimd.affine_select(out=ident[:, :], in_=ident[:, :], compare_op=ALU.not_equal, fill=1.0, base=0,
                                    pattern=[[-1, P]], channel_multiplier=1).then_inc(ident_ready, 1)
            for h in range(CH):
                pool.wait_ge(r0_scaled, h + 1)
                nc.gpsimd.tensor_tensor(mix0[:, R, h, :], mix0[:, R, h, :], xt0[:, h, 0:steps(0)],
                                        ALU.add).then_inc(r0_mixed, 1)
            mix_chunk(1)
            pool.wait_ge(wd_in, 16)
            nc.gpsimd.tensor_copy(wd_r[:, :, :], wd_i[:, :, :]).then_inc(wd_ready, 1)
            mix_v2()
            pool.wait_ge(wide_ready, 1)
            any_wide = pool.value_load(wide[0:1, 0:1], min_val=0, max_val=1)
            with pool.If(any_wide == 1):
                pool.wait_ge(squares_ready, 6)
                pool.wait_ge(wg_ready, 1)
                pool.wait_ge(wu_ready, 1)
                for w_int, w_f32 in ((wg_i, wg_f), (wu_i, wu_f), (wd_i, wd_f)):
                    nc.gpsimd.tensor_copy(w_f32, w_int[:, :, :]).then_inc(ffn_w_f32_ready, 1)
            round_(1, True, True)
            round_(2, True, True)
            with pool.Fori(3, NC - 2) as j:
                round_(j, True, True)
            round_(NC - 2, True, True)
            round_(NC - 1, True, False)
            for m in range(NP):
                low_part(NC - 1, m)

        @block.scalar
        def _(sc):
            def weight(c, i, h):
                sc.wait_ge(args_ready, c * (4 * CH) + (h * 4 + i + 1))
                old = i in (IN_OLD, OUT_OLD)
                n = steps(c)
                nc.scalar.activation(wts[:, i, h, 0:n], wts[:, i, h, 0:n], ACT.Exp,
                                     scale=-1.0 if old else 1.0).then_inc(wts_ready, 1)

            def scale_dx(c, i, h):
                sc.wait_ge(dx_ready, (c - 1) * CH + (h + 1))
                if not (isinstance(c, int) and c == 1):
                    sc.wait_ge([k_ready, v_ready, r_ready][i], c * CH)
                n = steps(c)
                nc.scalar.activation(mix[:, i, h, 0:n], dx[:, h, 0:n], ACT.Copy,
                                     scale=par[:, MIX + i, h:h + 1]).then_inc(dx_scaled, share(c, i, h))

            def scale_chunk(c, which=range(3)):
                for i in which:
                    for h in range(CH):
                        scale_dx(c, i, h)

            def norm1(c):
                if first(c) or last(c):
                    return
                sc.wait_ge(shift1_ready, c)
                sc.wait_ge(x1T_ready, c * CH)
                sc.wait_ge(res2_ready, c * 2)
                for q in range(steps(c) // P):
                    nc.scalar.activation(x1_of(c)[:, q, :], res1[:, q, :], ACT.Identity, bias=shift1[:, q:q + 1],
                                         scale=rstd1[:, q:q + 1]).then_inc(x1_ready, halved(c))

            def norm2(c, rows):
                if 0 in rows:
                    sc.wait_ge(shift2_ready, c + 1)
                    if not first(c):
                        sc.wait_ge(stored, c * 16)
                for q in rows:
                    nc.scalar.activation(y[:, q, :], res2[:, q, :], ACT.Identity, bias=shift2[:, q:q + 1],
                                         scale=rstd2[:, q:q + 1]).then_inc(y_ready, halved(c))

            def log_den(c, h):
                sc.wait_ge(den_ready, c * CH + (h + 1))
                n = steps(c)
                nc.scalar.activation(den[:, h, 0:n], den[:, h, 0:n], ACT.Ln, scale=2.0).then_inc(ln_ready, 1)

            def reciprocal(c, h):
                sc.wait_ge(ln_ready, c * CH + (h + 1))
                n = steps(c)
                nc.scalar.activation(den[:, h, 0:n], den[:, h, 0:n], ACT.Exp, scale=-1.0).then_inc(rec_ready, 1)

            def receptance(c, h):
                sc.wait_ge(r_ready, c * CH + (h + 1))
                if not first(c):
                    sc.wait_ge(gated, c * CH)
                n = steps(c)
                nc.scalar.activation(recv[:, h, 0:n], bank_c[:, h, 0:n], ACT.Tanh, scale=0.5).then_inc(recv_ready, 1)

            def rstd(c, mv, lnv, rs, mv_ready, lnv_ready, rstd_ready):
                sc.wait_ge(mv_ready, c * NT + NT)
                nt = steps(c) // P
                nc.scalar.activation(lnv[:, 0:nt], mv[:, 0:nt, 1], ACT.Ln, bias=eps[:, 0:1]).then_inc(lnv_ready, 1)
                sc.wait_ge(lnv_ready, c + 1)
                nc.scalar.activation(rs[:, 0:nt], lnv[:, 0:nt], ACT.Exp, scale=-0.5).then_inc(rstd_ready, 1)

            def x1_high(c, h):
                sc.wait_ge(x1T_ready, c * CH + (h + 1))
                if not first(c):
                    sc.wait_ge(up_ready, c * NM)
                n = steps(c)
                nc.scalar.activation(x1hi[:, h, 0:n], bank_b[:, h, 0:n], ACT.Copy).then_inc(x1hi_ready, 1)

            def silu(c, m):
                sc.wait_ge(gate_ready, c * NM + (m + 1))
                if not (first(c) and m < 2):
                    sc.wait_ge(hid_ready, c * NM + (m - 1))
                n = steps(c)
                nc.scalar.activation(act[:, m % 2, 0:n], gate_bank(c)[:, m % 2, 0:n], ACT.Silu,
                                     scale=SCALE).then_inc(act_ready, 1)

            def hid_high(c, m):
                sc.wait_ge(hid_ready, c * NM + (m + 1))
                if not first(c):
                    sc.wait_ge(ffn_ready, c * 2)
                n = steps(c)
                nc.scalar.activation(hhi[:, m, 0:n], hid[:, m % NH, 0:n], ACT.Copy).then_inc(hhi_ready, 1)

            def round_(j, ffn, nxt):
                sc.preload_act_table_set("silu_and_others")
                row_at = {1: 0, 2: 1, 3: 2, 4: 3} if not (isinstance(j, int) and j < 2) else {}
                for m in range(NM):
                    silu(j - 1, m)
                    if m == 0:
                        receptance(j, 0)
                    if m == 3:
                        receptance(j, 1)
                        hid_high(j - 1, m - 1)
                    if m in row_at and row_at[m] < steps(j - 2) // P:
                        norm2(j - 2, [row_at[m]])
                    if m not in (0, 3) and not (last(j) and m == NM - 1):
                        hid_high(j - 1, m - 1)
                sc.preload_act_table_set("natural_log_exp_and_others")
                log_den(j, 0)
                log_den(j, 1)
                if not last(j):
                    hid_high(j - 1, NM - 1)
                reciprocal(j, 0)
                reciprocal(j, 1)
                if last(j):
                    hid_high(j - 1, NM - 2)
                    hid_high(j - 1, NM - 1)
                if nxt:
                    scale_chunk(j + 1, (K, R) if isinstance(j, int) and j == 1 else range(3))
                first_norm(j, nxt)

            def first_norm(j, nxt):
                rstd(j, mv1, lnv1, rstd1, mv1_ready, lnv1_ready, rstd1_ready)
                if first(j):
                    nc.scalar.activation(wu_r[:, :, :], wu_i[:, :, :], ACT.Copy).then_inc(wu_ready, 1)
                norm1(j)
                if not first(j) and not last(j):
                    rstd(j - 1, mv2, lnv2, rstd2, mv2_ready, lnv2_ready, rstd2_ready)
                if nxt and not first(j):
                    weights(j + 1, 0, range(2))
                x1_high(j, 0)
                x1_high(j, 1)
                if nxt and not first(j):
                    weights(j + 1, 0, range(2, 4))
                if nxt:
                    weights(j + 1, 1)

            def range_check():
                for n, (w_int, w_in, half) in enumerate(((wg_i, wg_in, 1), (wu_i, wu_in, 1), (wd_i, wd_in, NM // 2))):
                    sc.wait_ge(w_in, 16)
                    for i in range(2):
                        if n + i > 0:
                            sc.wait_ge(squares_ready, 2 * n + i)
                        w_half = w_int[:, i * half:(i + 1) * half, :].rearrange("p a b -> p (a b)")
                        nc.scalar.activation(y[:, :, :].rearrange("p a b -> p (a b)")[:, 0:H], w_half, ACT.Square,
                                             scale=1.0 / EXACT,
                                             accum_out=squares[:, 2 * n + i:2 * n + i + 1]).then_inc(squares_ready, 1)

            def weights(c, h, which=range(4)):
                for i in which:
                    weight(c, i, h)

            nc.scalar.dma_start(par[:, :, :], params).then_inc(par_in, 16)
            nc.scalar.dma_start(wvT[:, :, :], wv.rearrange("(h p) d -> p h d", p=P)).then_inc(wv_in, 16)
            nc.scalar.dma_start(wrT[:, :, :], wr.rearrange("(h p) d -> p h d", p=P)).then_inc(wr_in, 16)
            sc.preload_act_table_set("exp_and_others")
            sc.wait_ge(par_in, 16)
            nc.scalar.activation(decay[:, :], par[:, DECAY, :], ACT.Exp).then_inc(decay_exp, 1)
            for h in range(CH):
                sc.wait_ge(dx0_ready, h + 1)
                nc.scalar.activation(mix0[:, R, h, :], dx0[:, h, :], ACT.Copy,
                                     scale=par[:, MIX + R, h:h + 1]).then_inc(r0_scaled, 1)
            weights(0, 0)
            scale_chunk(1, [K])
            weights(0, 1)
            receptance(0, 0)
            receptance(0, 1)
            sc.preload_act_table_set("natural_log_exp_and_others")
            scale_chunk(1, [V])
            for h in range(CH):
                log_den(0, h)
            for h in range(CH):
                reciprocal(0, h)
            scale_chunk(1, [R])
            sc.wait_ge(wg_in, 16)
            nc.scalar.activation(wg_r[:, :, :], wg_i[:, :, :], ACT.Copy).then_inc(wg_ready, 1)
            range_check()
            weights(1, 0)
            first_norm(0, True)
            round_(1, True, True)
            round_(2, True, True)
            with sc.Fori(3, NC - 2) as j:
                round_(j, True, True)
            round_(NC - 2, True, True)
            round_(NC - 1, True, False)
            sc.preload_act_table_set("silu_and_others")
            for m in range(NM):
                silu(NC - 1, m)
                if m > 0:
                    hid_high(NC - 1, m - 1)
            hid_high(NC - 1, NM - 1)
            sc.preload_act_table_set("natural_log_exp_and_others")
            rstd(NC - 2, mv2, lnv2, rstd2, mv2_ready, lnv2_ready, rstd2_ready)
            norm2(NC - 2, range(NT))
            rstd(NC - 1, mv2, lnv2, rstd2, mv2_ready, lnv2_ready, rstd2_ready)

        @block.vector
        def _(dve):
            def carry_max(c):
                if first(c):
                    return
                n = steps(c - 1)
                nc.vector.tensor_copy(pmax[:, :, 0:1], pmax[:, :, n:n + 1]).then_inc(pmax_carried, 1)

            def running_max(c, h):
                dve.wait_ge(k_ready, c * CH + (h + 1))
                if not first(c):
                    dve.wait_ge(pmax_carried, c)
                n = steps(c)
                nc.vector.tensor_tensor_scan(pmax[:, h, 1:n + 1], neg_decay[:, h:h + 1].broadcast_to([P, n]),
                                             bank_a[:, h, 0:n], pmax[:, h, 0:1], ALU.add,
                                             ALU.max).then_inc(pmax_ready, 1)

            def gaps(c, h):
                dve.wait_ge(pmax_ready, c * CH + (h + 1))
                n = steps(c)
                nc.vector.tensor_tensor(gap[:, h, 0:n], bank_a[:, h, 0:n], pmax[:, h, 0:n],
                                        ALU.subtract).then_inc(gap_ready, 1)

            def exp_args(c, h, which=range(4)):
                dve.wait_ge(gap_ready, c * CH + (h + 1))
                n = steps(c)
                for i in which:
                    s = decay[:, h:h + 1] if i in (IN_NEW, IN_OLD) else par[:, FIRST, h:h + 1]
                    op = ALU.max if i in (IN_OLD, OUT_OLD) else ALU.min
                    nc.vector.tensor_scalar(wts[:, i, h, 0:n], gap[:, h, 0:n], s, 0.0, ALU.add,
                                            op).then_inc(args_ready, 1)

            def weights_there(c, h):
                dve.wait_ge(wts_ready, c * (4 * CH) + (4 * h + 4))

            def carry_state(c):
                if first(c):
                    return
                n = steps(c - 1)
                nc.vector.tensor_copy(state[:, :, :, 0:1], state[:, :, :, n:n + 1]).then_inc(state_carried, 1)

            def scan_bb(c, h):
                weights_there(c, h)
                if not first(c):
                    dve.wait_ge(state_carried, c)
                n = steps(c)
                nc.vector.tensor_tensor_scan(state[:, 1, h, 1:n + 1], wts[:, IN_OLD, h, 0:n], wts[:, IN_NEW, h, 0:n],
                                             state[:, 1, h, 0:1], ALU.mult, ALU.add).then_inc(bb_ready, 1)

            def new_kv(c, h):
                dve.wait_ge(v_ready, c * CH + (h + 1))
                n = steps(c)
                nc.vector.tensor_tensor(kv[:, h, 0:n], wts[:, IN_NEW, h, 0:n], bank_d[:, h, 0:n],
                                        ALU.mult).then_inc(kv_ready, 1)

            def scan_aa(c, h):
                dve.wait_ge(kv_ready, c * CH + (h + 1))
                n = steps(c)
                nc.vector.tensor_tensor_scan(state[:, 0, h, 1:n + 1], wts[:, IN_OLD, h, 0:n], kv[:, h, 0:n],
                                             state[:, 0, h, 0:1], ALU.mult, ALU.add).then_inc(aa_ready, 1)

            def den_old(c, h):
                dve.wait_ge(bb_ready, c * CH + (h + 1))
                if not first(c):
                    dve.wait_ge(rwkv_ready, c * CH)
                n = steps(c)
                nc.vector.tensor_tensor(den[:, h, 0:n], wts[:, OUT_OLD, h, 0:n], state[:, 1, h, 0:n],
                                        ALU.mult).then_inc(den_part, 1)

            def den_sum(c, h):
                dve.wait_ge(den_part, c * CH + (h + 1))
                n = steps(c)
                nc.vector.tensor_tensor(den[:, h, 0:n], den[:, h, 0:n], wts[:, OUT_NEW, h, 0:n],
                                        ALU.add).then_inc(den_ready, 1)

            def num_old(c, h):
                dve.wait_ge(aa_ready, c * CH + (h + 1))
                n = steps(c)
                nc.vector.tensor_tensor(num[:, h, 0:n], wts[:, OUT_OLD, h, 0:n], state[:, 0, h, 0:n], ALU.mult)

            def num_new(c, h):
                n = steps(c)
                nc.vector.tensor_tensor(num2[:, h, 0:n], wts[:, OUT_NEW, h, 0:n], bank_d[:, h, 0:n],
                                        ALU.mult).then_inc(num_parts, 1)

            def numerator(c, h):
                dve.wait_ge(num_parts, c * CH + (h + 1))
                n = steps(c)
                nc.vector.tensor_tensor(num[:, h, 0:n], num[:, h, 0:n], num2[:, h, 0:n],
                                        ALU.add).then_inc(num_ready_dve, 1)

            def gate_num(c, h):
                if first(c):
                    dve.wait_ge(num_ready_dve, h + 1)
                elif last(c):
                    dve.wait_ge(num_ready_dve, CH + h + 1)
                else:
                    dve.wait_ge(num_ready, (c - 1) * CH + (h + 1))
                dve.wait_ge(recv_ready, c * CH + (h + 1))
                n = steps(c)
                nc.vector.scalar_tensor_tensor(out=num[:, h, 0:n], in0=recv[:, h, 0:n], scalar=1.0, in1=num[:, h, 0:n],
                                               op0=ALU.add, op1=ALU.mult).then_inc(gated, 1)

            def divide(c, h):
                dve.wait_ge(gated, c * CH + (h + 1))
                dve.wait_ge(rec_ready, c * CH + (h + 1))
                if not first(c):
                    dve.wait_ge(attn_ready, c * 2)
                n = steps(c)
                nc.vector.tensor_tensor(rwkv[:, h, 0:n], num[:, h, 0:n], den[:, h, 0:n],
                                        ALU.mult).then_inc(rwkv_ready, 1)

            def row_stats(c, res, stats, res_ready, stats_ready, tiles=None):
                for q in tiles or range(steps(c) // P):
                    if q % 2 == 0:
                        dve.wait_ge(res_ready, c * 2 + halved(c) * (q // 2 + 1))
                    nc.vector.bn_stats(stats[:, q, :], res[:, q, :]).then_inc(stats_ready, halved(c))

            def mean_var(c, stats, mv, mv_ready):
                for q in range(steps(c) // P):
                    nc.vector.bn_aggr(mv[:, q, :], stats[:, q, :]).then_inc(mv_ready, halved(c))

            def residual1_stats(c):
                dve.wait_ge(xrow_in, c * 16 + 16)
                if not first(c):
                    dve.wait_ge(x1_ready, c * NT)
                for b in range(2 // halved(c)):
                    dve.wait_ge(attn_ready, c * 2 + halved(c) * (b + 1))
                    nc.vector.tensor_tensor(res1[:, 2 * b:2 * b + 2, :], attn[:, 2 * b:2 * b + 2, :],
                                            xrow[:, 2 * b:2 * b + 2, :], ALU.add).then_inc(res1_ready, halved(c))
                    row_stats(c, res1, stats1, res1_ready, stats1_ready, (2 * b, 2 * b + 1))

            def norm_rows(c, out, res, mv, rs, rstd_ready, ready, count):
                dve.wait_ge(rstd_ready, c + 1)
                for q in range(steps(c) // P):
                    nc.vector.tensor_scalar(out[:, q, :], res[:, q, :], mv[:, q, 0:1], rs[:, q:q + 1],
                                            ALU.subtract, ALU.mult).then_inc(ready, count)

            def shift_rows1(c):
                dve.wait_ge(rstd1_ready, c + 1)
                nt = steps(c) // P
                nc.vector.scalar_tensor_tensor(out=shift1[:, 0:nt], in0=mv1[:, 0:nt, 0], scalar=-1.0, in1=rstd1[:, 0:nt],
                                               op0=ALU.mult, op1=ALU.mult).then_inc(shift1_ready, 1)

            def x1_low(c, h):
                dve.wait_ge(x1hi_ready, c * CH + (h + 1))
                if not first(c):
                    dve.wait_ge(up_ready, c * NM)
                n = steps(c)
                nc.vector.tensor_tensor(x1lo[:, h, 0:n], bank_b[:, h, 0:n], x1hi[:, h, 0:n].bitcast(f32),
                                        ALU.subtract).then_inc(x1lo_ready, 1)

            def product(c, m):
                dve.wait_ge(act_ready, c * NM + (m + 1))
                dve.wait_ge(up_ready, c * NM + (m + 1))
                if m >= NH:
                    dve.wait_ge(hlo_ready, c * NP + (m - NH + 1))
                elif m < NH - (NM - NP) and not first(c):
                    dve.wait_ge(hlo_ready, (c - 1) * NP + (m + NM - NH + 1))
                n = steps(c)
                nc.vector.tensor_tensor(hid[:, m % NH, 0:n], up_bank(c)[:, m % 2, 0:n], act[:, m % 2, 0:n],
                                        ALU.mult).then_inc(hid_ready, 1)

            def low_part(c, m):
                dve.wait_ge(hhi_ready, c * NM + (m + 1))
                if not first(c):
                    dve.wait_ge(ffn_ready, c * 2)
                n = steps(c)
                nc.vector.tensor_tensor(hlo[:, m, 0:n], hid[:, m % NH, 0:n], hhi[:, m, 0:n].bitcast(f32),
                                        ALU.subtract).then_inc(hlo_last_ready, 1)

            def residual2(c, banks=range(2)):
                if not first(c) and not last(c):
                    dve.wait_ge(y_ready, c * NT)
                for b in banks:
                    dve.wait_ge(ffn_ready, c * 2 + halved(c) * (b + 1))
                    nc.vector.scalar_tensor_tensor(out=(res2_last if last(c) else res2)[:, 2 * b:2 * b + 2, :], in0=ffn[:, 2 * b:2 * b + 2, :],
                                                   scalar=SCALE * SCALE, in1=x1_of(c)[:, 2 * b:2 * b + 2, :],
                                                   op0=ALU.mult, op1=ALU.add).then_inc(res2_ready, halved(c))

            def shift_rows2(c):
                dve.wait_ge(rstd2_ready, c + 1)
                nt = steps(c) // P
                nc.vector.scalar_tensor_tensor(out=shift2[:, 0:nt], in0=mv2[:, 0:nt, 0], scalar=-1.0, in1=rstd2[:, 0:nt],
                                               op0=ALU.mult, op1=ALU.mult).then_inc(shift2_ready, 1)

            def round_(j, ffn, nxt):
                def hidden(m):
                    if ffn:
                        product(j - 1, m)
                if not (isinstance(j, int) and j == 1):
                    begin_recurrence(j)
                scan_bb(j, 1)
                new_kv(j, 1)
                scan_aa(j, 0)
                hidden(0)
                scan_aa(j, 1)
                hidden(1)
                den_old(j, 0)
                den_old(j, 1)
                hidden(2)
                num_old(j, 0)
                num_old(j, 1)
                hidden(3)
                num_new(j, 0)
                num_new(j, 1)
                hidden(4)
                den_sum(j, 0)
                den_sum(j, 1)
                if first(j) or last(j):
                    numerator(j, 0)
                    numerator(j, 1)
                if last(j):
                    gate_num(j, 0)
                    gate_num(j, 1)
                    hidden(5)
                    divide(j, 0)
                    divide(j, 1)
                    low_part(j - 1, NM - 2)
                    low_part(j - 1, NM - 1)
                else:
                    hidden(5)
                    gate_num(j, 0)
                    if ffn:
                        low_part(j - 1, NM - 2)
                    gate_num(j, 1)
                    if ffn:
                        low_part(j - 1, NM - 1)
                    divide(j, 0)
                    divide(j, 1)
                if last(j):
                    norm_stats1(j)
                    norm_rows(j, x1_last, res1, mv1, rstd1, rstd1_ready, x1_ready, halved(j))
                    residual2(j - 1, [0])
                    x1_low(j, 0)
                    x1_low(j, 1)
                    residual2(j - 1, [1])
                    return
                if first(j):
                    next_max(1)
                    exp_args(1, 0)
                    norm_stats1(0)
                    range_flag()
                    exp_args(1, 1, [0, 1])
                    wide_flag()
                    exp_args(1, 1, [2])
                    norm_rows(0, x1, res1, mv1, rstd1, rstd1_ready, x1_ready, halved(0))
                    exp_args(1, 1, [3])
                    x1_low(0, 0)
                    x1_low(0, 1)
                    begin_recurrence(1)
                    return
                residual2(j - 1, range(2 // halved(j - 1)))
                row_stats(j - 1, res2, stats2, res2_ready, stats2_ready)
                dve.wait_ge(stats2_ready, (j - 1) * NT + NT)
                residual1_stats(j)
                dve.wait_ge(stats1_ready, j * NT + NT)
                carry_max(j + 1)
                mean_var(j, stats1, mv1, mv1_ready)
                mean_var(j - 1, stats2, mv2, mv2_ready)
                running_max(j + 1, 0)
                shift_rows1(j)
                running_max(j + 1, 1)
                gaps(j + 1, 0)
                gaps(j + 1, 1)
                exp_args(j + 1, 0)
                shift_rows2(j - 1)
                exp_args(j + 1, 1, (IN_NEW, IN_OLD))
                x1_low(j, 0)
                x1_low(j, 1)
                exp_args(j + 1, 1, (OUT_OLD, OUT_NEW))

            def range_flag():
                dve.wait_ge(squares_ready, 6)
                nc.vector.tensor_reduce(squares_max[:, :], squares[:, :], mybir.AxisListType.X,
                                        ALU.max).then_inc(squares_max_ready, 1)
                dve.wait_ge(squares_max_ready, 1)
                nc.vector.tensor_scalar(out_of_range[:, :], squares_max[:, :], 1.0, None,
                                        ALU.is_gt).then_inc(out_of_range_ready, 1)

            def wide_flag():
                dve.wait_ge(out_of_range_total, 1)
                nc.vector.tensor_scalar(wide[:, :], bank_b[0:1, 1, 0:1], 1.0, None, ALU.min).then_inc(wide_ready, 1)

            def begin_recurrence(c):
                carry_state(c)
                scan_bb(c, 0)
                new_kv(c, 0)

            def next_max(c):
                carry_max(c)
                running_max(c, 0)
                running_max(c, 1)
                gaps(c, 0)
                gaps(c, 1)

            def norm_stats1(c):
                residual1_stats(c)
                dve.wait_ge(stats1_ready, c * NT + NT)
                mean_var(c, stats1, mv1, mv1_ready)

            nc.vector.memset(eps[:, :], EPS)
            nc.vector.memset(zeros[:, :], 0.0).then_inc(zeros_ready, 1)
            nc.vector.memset(ones[:, :], 1.0)
            nc.vector.memset(pmax[:, :, 0:1], START)
            nc.vector.memset(state[:, :, :, 0:1], 0.0).then_inc(consts_ready, 1)
            def mix0_step(i, h):
                dve.wait_ge(dx0_ready, h + 1)
                nc.vector.scalar_tensor_tensor(out=mix0[:, i, h, :], in0=dx0[:, h, :],
                                               scalar=par[:, MIX + i, h:h + 1], in1=xt0[:, h, 0:steps(0)],
                                               op0=ALU.mult, op1=ALU.add).then_inc(kv0_mixed, 1)

            dve.wait_ge(xt0_in, 16)
            for h in range(CH):
                nc.vector.tensor_tensor(dx0[:, h, :], xt0[:, h, 1:steps(0) + 1], xt0[:, h, 0:steps(0)],
                                        ALU.subtract).then_inc(dx0_ready, 1)
                if h == 0:
                    dve.wait_ge(par_in, 16)
                mix0_step(K, h)
            mix0_step(V, 0)
            mix0_step(V, 1)
            dve.wait_ge(decay_exp, 1)
            nc.vector.tensor_scalar(neg_decay[:, :], decay[:, :], -1.0, None, ALU.mult).then_inc(decay_ready, 1)
            dve.wait_ge(consts_ready, 1)
            dve.wait_ge(decay_ready, 1)
            for h in range(CH):
                running_max(0, h)
                gaps(0, h)
                exp_args(0, h)
            round_(0, False, True)
            round_(1, True, True)
            round_(2, True, True)
            with dve.Fori(3, NC - 2) as j:
                round_(j, True, True)
            round_(NC - 2, True, True)
            round_(NC - 1, True, False)
            for m in range(NM):
                product(NC - 1, m)
                if m in (1, 2, 3, 4):
                    row_stats(NC - 2, res2, stats2, res2_ready, stats2_ready, [m - 1])
            dve.wait_ge(stats2_ready, (NC - 1) * NT)
            mean_var(NC - 2, stats2, mv2, mv2_ready)
            low_part(NC - 1, NM - 2)
            low_part(NC - 1, NM - 1)
            shift_rows2(NC - 2)
            residual2(NC - 1, [0])
            row_stats(NC - 1, res2_last, stats2, res2_ready, stats2_ready)
            dve.wait_ge(stats2_ready, NC * NT)
            mean_var(NC - 1, stats2, mv2, mv2_ready)
            norm_rows(NC - 1, y_last, res2_last, mv2, rstd2, rstd2_ready, y_last_ready, 1)

        @block.tensor
        def _(pe):
            def keep_warm(bank, times):
                for _ in range(times):
                    nc.tensor.matmul(bank[:, 0, 0:C], zeros[:, 0:P], zeros[:, :], start=True, stop=True)

            def project(c, i, halves=range(CH)):
                w, bank, ready = ((wkT, bank_a, k_ready), (wvT, bank_d, v_ready), (wrT, bank_c, r_ready))[i]
                if first(c):
                    mixed0 = r0_mixed if i == R else kv0_mixed
                    before = 0 if i == R else i * CH
                    pe.wait_ge(mixed0, before + 1)
                elif isinstance(c, int) and c == 2 and i == V:
                    pe.wait_ge(v2_mixed, CH)
                else:
                    pe.wait_ge(mixed, (c - 1) * (3 * CH) + (i + 1) * CH)
                n = steps(c)
                mixed_x = mix0 if first(c) else mix
                if not first(c):
                    if i == K:
                        pe.wait_ge(gap_ready, c * CH)
                        if not (isinstance(c, int) and c < 2):
                            pe.wait_ge(res2_ready, (c - 1) * 2)
                    elif i == V:
                        pe.wait_ge(num_parts, c * CH)
                for d in halves:
                    if i == R and not first(c):
                        pe.wait_ge(recv_ready, (c - 1) * CH + (d + 1))
                    for h in range(CH):
                        if first(c) and d == 0 and h > 0:
                            pe.wait_ge(mixed0, before + h + 1)
                        mm = nc.tensor.matmul(bank[:, d, 0:n], w[:, h, d * P:(d + 1) * P], mixed_x[:, i, h, 0:n],
                                              start=(h == 0), stop=(h == CH - 1))
                    mm.then_inc(ready, 1)

            def attention_out(c):
                pe.wait_ge(rwkv_ready, c * CH + CH)
                if not first(c):
                    pe.wait_ge(hid_ready, c * NM)
                for q in range(steps(c) // P):
                    for h in range(CH):
                        mm = nc.tensor.matmul(attn[:, q, :], rwkv[:, h, q * P:(q + 1) * P], woT[:, h, :],
                                              start=(h == 0), stop=(h == CH - 1))
                    if q % 2 == 1:
                        mm.then_inc(attn_ready, halved(c))

            def transpose_x1(c):
                pe.wait_ge(x1_ready, c * NT + NT)
                for h in range(CH):
                    for q in range(steps(c) // P):
                        mm = nc.tensor.transpose(bank_b[:, h, q * P:(q + 1) * P], x1_of(c)[:, q, h * P:(h + 1) * P],
                                                 ident[:, :])
                    mm.then_inc(x1T_ready, 1)

            def gate_up(c, tiles, full):
                if 0 in tiles:
                    if first(c):
                        pe.wait_ge(gap_ready, 2 * CH)
                    elif not last(c):
                        pe.wait_ge(gap_ready, c * CH + 2 * CH)
                for m in tiles:
                    for w, bank, ready in ((wg_f if full else wg_r, gate_bank(c), gate_ready),
                                           (wu_f if full else wu_r, up_bank(c), up_ready)):
                        if not (first(c) and m < 2):
                            pe.wait_ge(act_ready if ready is gate_ready else hid_ready, c * NM + (m - 1))
                        for part, part_ready in ((x1hi, x1hi_ready), (x1lo, x1lo_ready)):
                            for h in range(CH):
                                if m == 0 and ready is gate_ready:
                                    pe.wait_ge(part_ready, c * CH + (h + 1))
                                xp = part[:, h, 0:steps(c)]
                                if full:
                                    xp = xp.bitcast(f32)
                                mm = nc.tensor.matmul(bank[:, m % 2, 0:steps(c)], w[:, h, m * P:(m + 1) * P], xp,
                                                      start=(h == 0 and part is x1hi),
                                                      stop=(h == CH - 1 and part is x1lo))
                        mm.then_inc(ready, 1)

            def down(c, tiles, full):
                w = wd_f if full else wd_r
                if 0 in tiles:
                    if last(c):
                        pe.wait_ge(res2_ready, c * 2)
                    else:
                        pe.wait_ge(act_ready, c * NM + NM)
                for m in tiles:
                    pe.wait_ge(hhi_ready, c * NM + (m + 1))
                    if m < NP:
                        pe.wait_ge(hlo_ready, c * NP + (m + 1))
                    else:
                        pe.wait_ge(hlo_last_ready, c * (NM - NP) + (m - NP + 1))
                    for q in range(steps(c) // P):
                        for part in (hhi, hlo):
                            hp = part[:, m, q * P:(q + 1) * P]
                            mm = nc.tensor.matmul(ffn[:, q, :], hp.bitcast(f32) if full else hp, w[:, m, :],
                                                  start=(m == 0 and q % 2 == 0 and part is hhi),
                                                  stop=(m == NM - 1 and part is hlo), skip_group_check=True)
                        if m == NM - 1 and q % 2 == 1:
                            mm.then_inc(ffn_ready, halved(c))

            def ffn_products(j, full):
                if full:
                    pe.wait_ge(ffn_w_f32_ready, 3)
                gate_up(j - 1, range(2), full)
                gate_up(j - 1, range(2, NM), full)
                if last(j):
                    down(j - 1, range(NM // 2), full)
                    attention_out(j)
                    down(j - 1, range(NM // 2, NM), full)
                elif isinstance(j, int) and j == 1:
                    down(0, range(3), full)
                    project(2, V)
                    down(0, range(3, NM), full)
                else:
                    down(j - 1, range(NM), full)

            def round_(j, ffn, nxt):
                if ffn:
                    with pe.If(any_wide == 0):
                        ffn_products(j, False)
                    with pe.Else():
                        ffn_products(j, True)
                if nxt and first(j):
                    project(j + 1, K)
                    project(j + 1, V)
                    pe.wait_ge(wo_in, 16)
                if not last(j):
                    attention_out(j)
                if nxt and not first(j):
                    project(j + 1, K)
                    if not (isinstance(j, int) and j == 1):
                        project(j + 1, V)
                if first(j) or last(j + 1):
                    project(j + 1, R)
                if isinstance(j, int) and j == 1:
                    project(j + 1, R, [0])
                if first(j):
                    pe.wait_ge(out_of_range_ready, 1)
                    nc.tensor.matmul(bank_b[0:1, 1, 0:1], ones[:, :], out_of_range[:, :],
                                     start=True, stop=True).then_inc(out_of_range_total, 1)
                    pe.wait_ge(wide_ready, 1)
                    pe.wait_ge(ident_ready, 1)
                    pe.wait_ge(gap_ready, 2 * CH)
                    keep_warm(bank_a, 4)
                if last(j):
                    pe.wait_ge(recv_ready, NC * CH)
                    keep_warm(bank_c, 2)
                transpose_x1(j)
                if first(j):
                    keep_warm(bank_a, 2)
                if nxt and not first(j) and not last(j + 1):
                    project(j + 1, R, [1] if isinstance(j, int) and j == 1 else range(CH))

            pe.wait_ge(zeros_ready, 1)
            keep_warm(bank_c, 4)
            pe.wait_ge(wk_in, 16)
            project(0, K)
            pe.wait_ge(wv_in, 16)
            project(0, V)
            pe.wait_ge(wr_in, 16)
            project(0, R)
            round_(0, False, True)
            any_wide = pe.value_load(wide[0:1, 0:1], min_val=0, max_val=1)
            pe.wait_ge(wg_ready, 1)
            pe.wait_ge(wu_ready, 1)
            pe.wait_ge(wd_ready, 1)
            round_(1, True, True)
            round_(2, True, True)
            with pe.Fori(3, NC - 2) as j:
                round_(j, True, True)
            round_(NC - 2, True, True)
            round_(NC - 1, True, False)
            with pe.If(any_wide == 0):
                ffn_products(NC, False)
            with pe.Else():
                ffn_products(NC, True)


def kernel(**inputs):
    import numpy as np
    import concourse.bacc as bacc
    from concourse.bass_utils import run_bass_kernel_spmd

    a = {k[3:]: np.asarray(v) for k, v in inputs.items()}
    x = a["attn_x"][0]
    xT = np.zeros((x.shape[1], x.shape[0] + 1), x.dtype)
    xT[:, 1:] = x.T
    arrays = {
        "xT": xT,
        "x": x,
        "params": np.stack([a["attn_time_decay"], a["attn_time_first"], a["attn_time_mix_k"].reshape(-1),
                            a["attn_time_mix_v"].reshape(-1), a["attn_time_mix_r"].reshape(-1)])
                  .reshape(5, -1, 128).transpose(2, 0, 1),
        "wk": a["attn_Wk"].T, "wv": a["attn_Wv"].T, "wr": a["attn_Wr"].T, "wo": a["attn_Wo"].T,
        "wg": a["ffn_w_gate"].T, "wu": a["ffn_w_up"].T, "wd": a["ffn_w_down"].T,
    }
    arrays = {k: np.ascontiguousarray(v) for k, v in arrays.items()}
    nc = bacc.Bacc("TRN2", target_bir_lowering=False, num_devices=1)
    args = [nc.dram_tensor(k, v.shape, mybir.dt.from_np(v.dtype), kind="ExternalInput").ap()
            for k, v in arrays.items()]
    out = nc.dram_tensor("out", x.shape, mybir.dt.float32, kind="ExternalOutput").ap()
    rwkv_swiglu_kernel(nc, *args, out)
    r = run_bass_kernel_spmd(nc, [arrays], core_ids=[0])
    return np.asarray(r.results[0]["out"]).reshape(1, *x.shape)
```
